# Optimizing a Trainium2 kernel written in Bass

```python
import numpy as np
import jax
import jax.numpy as jnp

def _softmax(x, axis=-1):
    return jax.nn.softmax(x, axis=axis)

def _gelu(x):
    return jax.nn.gelu(x, approximate=True)

def _silu(x):
    return jax.nn.silu(x)

def _sigmoid(x):
    return jax.nn.sigmoid(x)

def _layernorm(x, axis=-1, eps=1e-05):
    m = jnp.mean(x, axis=axis, keepdims=True)
    v = jnp.var(x, axis=axis, keepdims=True)
    return (x - m) / jnp.sqrt(v + eps)

def _scatter_add(tgt, idx, src, axis=0):
    return tgt.at[idx].add(src)

def _segment_sum(src, seg, n):
    return jax.ops.segment_sum(src, seg, n)
kernel_name = 'mk_gnn_preln_d2_gnn_r32_90ce99'

def setup_inputs(seed: int=0):
    np.random.seed(seed)
    _w = jnp.asarray

    def _rec_inputs():
        import jax
        import jax.numpy as jnp
        _gk = jax.random.key(seed)
        x = -0.0003713 + 1 * jax.random.normal(jax.random.fold_in(_gk, 1), (3125, 128), jnp.float32)
        _s = jax.random.randint(jax.random.fold_in(_gk, 2), (25000,), 0, 3125, jnp.int32)
        _d = jax.random.randint(jax.random.fold_in(_gk, 3), (25000,), 0, 3125, jnp.int32)
        _loop = jnp.arange(3125, dtype=jnp.int32)
        src = jnp.concatenate([_s, _d, _loop])
        dst = jnp.concatenate([_d, _s, _loop])
        _o = jnp.argsort(dst, stable=True)
        src = src[_o]
        dst = dst[_o]
        edge_attr_64 = -5.16925e-05 + 1.00005 * jax.random.normal(jax.random.fold_in(_gk, 11), (53125, 64), jnp.float32)
        edge_weight = jax.random.uniform(jax.random.fold_in(_gk, 13), (53125,), jnp.float32, 0.0, 0.999999)
        return (x, src, dst, edge_attr_64, edge_weight)
    x, src, dst, edge_attr_64, edge_weight = _rec_inputs()

    def _L0_gnn_setup():
        import jax, jax.numpy as jnp
        import numpy as np
        N_NODES = 3125
        N_EDGES = 50000
        IN_CH = 128
        OUT_CH = 128
        EDGE_DIM = 64
        key = jax.random.key(seed)
        ks = jax.random.split(key, 7)
        x = jax.random.normal(ks[0], (N_NODES, IN_CH), dtype=jnp.float32)
        edge_index = jax.random.randint(ks[1], (2, N_EDGES), 0, N_NODES, dtype=jnp.int64)
        edge_attr = jax.random.normal(ks[2], (N_EDGES, EDGE_DIM), dtype=jnp.float32)
        lim1 = 1.0 / np.sqrt(IN_CH)
        W_lin = jax.random.uniform(ks[3], (IN_CH, OUT_CH), minval=-lim1, maxval=lim1, dtype=jnp.float32)
        b_lin = jax.random.uniform(ks[4], (OUT_CH,), minval=-lim1, maxval=lim1, dtype=jnp.float32)
        lim2 = 1.0 / np.sqrt(EDGE_DIM)
        W_edge = jax.random.uniform(ks[5], (EDGE_DIM, OUT_CH), minval=-lim2, maxval=lim2, dtype=jnp.float32)
        b_edge = jax.random.uniform(ks[6], (OUT_CH,), minval=-lim2, maxval=lim2, dtype=jnp.float32)
        return {'x': x, 'edge_index': edge_index, 'edge_attr': edge_attr, 'W_lin': W_lin, 'b_lin': b_lin, 'W_edge': W_edge, 'b_edge': b_edge}
    _L0_gnn_all = _L0_gnn_setup()
    _L0_gnn_in = {k: v for k, v in _L0_gnn_all.items() if k in ('W_lin', 'b_lin', 'W_edge', 'b_edge')}
    del _L0_gnn_all

    def _L1_gnn_setup():
        import jax, jax.numpy as jnp
        import numpy as np
        N_NODES = 3125

        def gcn_conv(h, row, col, w, W, b, n):
            h = h @ W
            deg = jax.ops.segment_sum(w, row, num_segments=n)
            dinv = jnp.where(deg > 0, jax.lax.rsqrt(deg), 0.0)
            norm = dinv[row] * w * dinv[col]
            msg = norm[:, None] * h[col]
            return jax.ops.segment_sum(msg, row, num_segments=n) + b
        key = jax.random.key(seed)
        ks = jax.random.split(key, 6)
        N, E, D, H = (N_NODES, 50000, 128, 128)
        x = jax.random.normal(ks[0], (N, D), dtype=jnp.float32)
        edge_index = jax.random.randint(ks[1], (2, E), 0, N, dtype=jnp.int64)
        edge_weight = jax.random.uniform(ks[2], (E,), dtype=jnp.float32)
        W1 = jax.random.normal(ks[3], (D, H), dtype=jnp.float32) / np.sqrt(D)
        b1 = jnp.zeros((H,), dtype=jnp.float32)
        W2 = jax.random.normal(ks[4], (H, H), dtype=jnp.float32) / np.sqrt(H)
        b2 = jnp.zeros((H,), dtype=jnp.float32)
        return {'x': x, 'edge_index': edge_index, 'edge_weight': edge_weight, 'W1': W1, 'b1': b1, 'W2': W2, 'b2': b2}
    _L1_gnn_all = _L1_gnn_setup()
    _L1_gnn_in = {k: v for k, v in _L1_gnn_all.items() if k in ('W1', 'b1', 'W2', 'b2')}
    del _L1_gnn_all
    return {'x': x, 'src': src, 'dst': dst, 'edge_attr_64': edge_attr_64, 'edge_weight': edge_weight, 'L0_gnn_W_lin': _L0_gnn_in['W_lin'], 'L0_gnn_b_lin': _L0_gnn_in['b_lin'], 'L0_gnn_W_edge': _L0_gnn_in['W_edge'], 'L0_gnn_b_edge': _L0_gnn_in['b_edge'], 'L1_gnn_W1': _L1_gnn_in['W1'], 'L1_gnn_b1': _L1_gnn_in['b1'], 'L1_gnn_W2': _L1_gnn_in['W2'], 'L1_gnn_b2': _L1_gnn_in['b2']}

def reference(x, src, dst, edge_attr_64, edge_weight, L0_gnn_W_lin, L0_gnn_b_lin, L0_gnn_W_edge, L0_gnn_b_edge, L1_gnn_W1, L1_gnn_b1, L1_gnn_W2, L1_gnn_b2):
    import jax
    import jax.numpy as jnp

    def _L0_gnn_ref(x, edge_index, edge_attr, W_lin, b_lin, W_edge, b_edge):
        import jax, jax.numpy as jnp
        import numpy as np
        N_NODES = 3125
        N_EDGES = 50000
        IN_CH = 128
        OUT_CH = 128
        EDGE_DIM = 64
        h = x @ W_lin + b_lin
        row, col = (edge_index[0], edge_index[1])
        x_j = h[col]
        msg = x_j + (edge_attr @ W_edge + b_edge)
        aggr = jax.ops.segment_sum(msg, row, num_segments=h.shape[0])
        return jax.nn.relu(aggr)

    def _L1_gnn_ref(x, edge_index, edge_weight, W1, b1, W2, b2):
        import jax, jax.numpy as jnp
        import numpy as np
        N_NODES = 3125

        def gcn_conv(h, row, col, w, W, b, n):
            h = h @ W
            deg = jax.ops.segment_sum(w, row, num_segments=n)
            dinv = jnp.where(deg > 0, jax.lax.rsqrt(deg), 0.0)
            norm = dinv[row] * w * dinv[col]
            msg = norm[:, None] * h[col]
            return jax.ops.segment_sum(msg, row, num_segments=n) + b
        n = x.shape[0]
        loops = jnp.arange(n, dtype=edge_index.dtype)
        row = jnp.concatenate([edge_index[0], loops])
        col = jnp.concatenate([edge_index[1], loops])
        w = jnp.concatenate([edge_weight, jnp.ones((n,), dtype=edge_weight.dtype)])
        h = gcn_conv(x, row, col, w, W1, b1, n)
        h = jax.nn.relu(h)
        h = gcn_conv(h, row, col, w, W2, b2, n)
        return h
    edge_index = jnp.stack([src, dst])
    h = jnp.maximum(_layernorm(x, axis=-1), 0.0)
    x = x + _L0_gnn_ref(h, edge_index, edge_attr_64, L0_gnn_W_lin, L0_gnn_b_lin, L0_gnn_W_edge, L0_gnn_b_edge)
    h = jnp.maximum(_layernorm(x, axis=-1), 0.0)
    x = x + _L1_gnn_ref(h, edge_index, edge_weight, L1_gnn_W1, L1_gnn_b1, L1_gnn_W2, L1_gnn_b2)
    return x

_drawn_inputs = setup_inputs


def setup_inputs(seed=0):
    import zlib

    import numpy as np

    out = dict(_drawn_inputs(seed))
    spreads = {'L1_gnn_b1': (0.0, 0.466), 'L1_gnn_b2': (0.0, 0.274)}
    factors = {'edge_weight': 6.065}
    for name, (base, spread) in spreads.items():
        noise = np.random.default_rng([zlib.crc32(name.encode()), seed]).standard_normal(out[name].shape)
        drawn = base * np.exp(spread * noise) if base else spread * noise
        out[name] = jnp.asarray(drawn.astype(out[name].dtype))
    for name, factor in factors.items():
        out[name] = (out[name] * factor).astype(out[name].dtype)
    return out
```

```python
from contextlib import ExitStack

import concourse.bass as bass
from concourse import mybir

F32 = mybir.dt.float32
BF16 = mybir.dt.bfloat16
I32 = mybir.dt.int32
ALU = mybir.AluOpType
ACT = mybir.ActivationFunctionType

P = 128
BANK = 512


def build_graph_layers(nc, x, src, dst, edge_attr, edge_weight, W_lin, b_lin, W_edge, b_edge,
                       W1, b1, W2, b2, out):
    N, D = x.shape
    E, DE = edge_attr.shape
    T = -(-N // P)
    NP = T * P
    NR = N - (T - 1) * P
    C = -(-E // P)
    ER = E - (C - 1) * P
    K = 4
    PL = C // K
    LROW = K * P
    LR = E - (PL - 1) * LROW
    DX = DE + 2
    NB = -(-NP // BANK)
    EPS = 1e-5
    assert C % K == 0 and PL <= P and D == P and DX <= P

    table = nc.dram_tensor("node_table", [NP, D], F32, kind="Internal").ap()

    with ExitStack() as ctx:
        def sb(name, shape, dt=F32):
            return ctx.enter_context(nc.sbuf_tensor(name, shape, dt))

        def sem(name):
            return ctx.enter_context(nc.semaphore(name))

        x_sb = sb("x_sb", [P, T, D])
        z_sb = sb("z_sb", [P, T, D])
        sumT = sb("sumT", [P, NP])
        edgeT = sb("edgeT", [P, NP])
        iota_n = sb("iota_n", [P, NP])
        onehot = sb("onehot", [P, 2, NP])
        ident = sb("ident", [P, P])
        zeros = sb("zeros", [P, BANK])
        ones_col = sb("ones_col", [P, 1])
        listI = sb("listI", [P, 2, LROW], I32)
        listF = sb("listF", [P, 3, LROW])
        meta = sb("meta", [P, C, 3])
        slotF = sb("slotF", [P, 2, 3])
        slotI = sb("slotI", [P, 2, 1], I32)
        erow = sb("erow", [P, 2, DX])
        gath = sb("gath", [P, 2, D])
        msg = sb("msg", [P, 2, D])
        wl = sb("wl", [P, D])
        we = sb("we", [P, D])
        be = sb("be", [P, D])
        w1 = sb("w1", [P, D])
        w2 = sb("w2", [P, D])
        b1s = sb("b1s", [P, D])
        b2s = sb("b2s", [P, D])
        stats = sb("stats", [P, T, 6])
        mv = sb("mv", [P, T, 2])
        std = sb("std", [P, T])
        rstd = sb("rstd", [P, T])
        deg = sb("deg", [P, T])
        degpos = sb("degpos", [P, T])
        dinv = sb("dinv", [P, T])
        sel = sb("sel", [P, 1])
        acc = ctx.enter_context(nc.psum_tensor("acc", [P, NB * BANK], F32))
        misc = ctx.enter_context(nc.psum_tensor("misc", [P, BANK], F32))

        x_in = sem("x_in")
        lists_in = sem("lists_in")
        weights_in = sem("weights_in")
        pads_set = sem("pads_set")
        consts = sem("consts")
        zeroed = sem("zeroed")
        lists_f = sem("lists_f")
        lists_t = sem("lists_t")
        meta_ready = sem("meta_ready")
        ln_var = sem("ln_var")
        ln_std = sem("ln_std")
        z_ready = sem("z_ready")
        table_out = sem("table_out")
        erow_in = [sem(f"erow_in{k}") for k in range(2)]
        ew_ready = sem("ew_ready")
        idx_ready = sem("idx_ready")
        gath_in = [sem(f"gath_in{k}") for k in range(2)]
        msg_ready = sem("msg_ready")
        oh_ready = sem("oh_ready")
        chunk_done = sem("chunk_done")
        sum_done = sem("sum_done")
        sum_copied = sem("sum_copied")
        deg_done = sem("deg_done")
        proj_done = sem("proj_done")
        deg_safe = sem("deg_safe")
        deg_sqrt = sem("deg_sqrt")
        out_ready = sem("out_ready")
        out_done = sem("out_done")
        dve_chain = sem("dve_chain")
        pool_chain = sem("pool_chain")
        pool_turn = sem("pool_turn")

        HALF = C // 2
        block = ctx.enter_context(nc.Block())

        @block.sync
        def _(sp):
            sp.dma_start(x_sb[:, 0:T - 1, :], x[0:(T - 1) * P, :].rearrange("(t p) f -> p t f", p=P)).then_inc(x_in, 16)
            sp.wait_ge(pads_set, 5)
            sp.dma_start(x_sb[0:NR, T - 1, :], x[(T - 1) * P:N, :]).then_inc(x_in, 16)
            full = (PL - 1) * LROW
            for f, a in enumerate((src, dst)):
                sp.dma_start(listI[0:PL - 1, f, :], a[0:full].rearrange("(p n) -> p n", n=LROW)).then_inc(lists_in, 16)
                sp.dma_start(listI[PL - 1:PL, f, 0:LR], a[full:E].rearrange("(p n) -> p n", p=1)).then_inc(lists_in, 16)
            sp.dma_start(listF[0:PL - 1, 2, :], edge_weight[0:full].rearrange("(p n) -> p n", n=LROW)).then_inc(lists_in, 16)
            sp.dma_start(listF[PL - 1:PL, 2, 0:LR], edge_weight[full:E].rearrange("(p n) -> p n", p=1)).then_inc(lists_in, 16)
            sp.dma_start(wl[:, :], W_lin).then_inc(weights_in, 16)
            sp.dma_start(w1[:, :], W1).then_inc(weights_in, 16)
            sp.dma_start(w2[:, :], W2).then_inc(weights_in, 16)
            sp.dma_start(we[0:DE, :], W_edge).then_inc(weights_in, 16)
            sp.dma_start(we[DE:DE + 1, :], b_lin.rearrange("(a d) -> a d", a=1)).then_inc(weights_in, 16)
            sp.dma_start(be[DE:DE + 1, :], b_edge.rearrange("(a d) -> a d", a=1)).then_inc(weights_in, 16)
            sp.dma_start(b1s[:, :], b1.rearrange("(a d) -> a d", a=1).broadcast_to([P, D])).then_inc(weights_in, 16)
            sp.dma_start(b2s[:, :], b2.rearrange("(a d) -> a d", a=1).broadcast_to([P, D])).then_inc(weights_in, 16)

            with sp.Fori(0, HALF - 1) as i:
                for k in range(2):
                    sp.wait_ge(chunk_done, 2 * i + k + 1)
                    sp.dma_start(erow[:, k, 0:DE], edge_attr[bass.ds(i * (2 * P) + k * P, P), :]).then_inc(erow_in[k], 16)
            sp.wait_ge(chunk_done, C - 1)
            sp.dma_start(erow[:, 0, 0:DE], edge_attr[(C - 2) * P:(C - 1) * P, :]).then_inc(erow_in[0], 16)
            sp.wait_ge(chunk_done, C)
            sp.dma_start(erow[0:ER, 1, 0:DE], edge_attr[(C - 1) * P:E, :]).then_inc(erow_in[1], 16)

            tview = table.rearrange("(t p) f -> p t f", p=P)
            for r in range(3):
                sp.wait_ge(z_ready, r + 1)
                if r:
                    sp.wait_ge(sum_done, r + 1)
                sp.dma_start(tview, z_sb[:, :, :]).then_inc(table_out, 16)
                sp.wait_ge(table_out, 16 * (r + 1))
            sp.wait_ge(out_ready, 1)
            sp.dma_start(out[0:(T - 1) * P, :].rearrange("(t p) f -> p t f", p=P), z_sb[:, 0:T - 1, :]).then_inc(out_done, 16)
            sp.dma_start(out[(T - 1) * P:N, :], z_sb[0:NR, T - 1, :]).then_inc(out_done, 16)
            sp.wait_ge(out_done, 32)

        @block.gpsimd
        def _(pool):
            pool.memset(x_sb[:, T - 1, :], 0.0).then_inc(pads_set, 1)
            pool.memset(listI[:, 0, :], -1).then_inc(pads_set, 1)
            pool.memset(listI[:, 1, :], 0).then_inc(pads_set, 1)
            pool.memset(listF[:, 2, :], 0.0).then_inc(pads_set, 1)
            pool.memset(we[:, :], 0.0).then_inc(pads_set, 1)
            pool.iota(iota_n[:, :], [[1, NP]], base=0, channel_multiplier=0,
                      allow_small_or_imprecise_dtypes=True).then_inc(consts, 1)
            pool.memset(ident[:, :], 0.0).then_inc(pool_chain, 1)
            pool.memset(sel[:, :], 0.0).then_inc(pool_chain, 1)
            pool.wait_ge(pool_chain, 2)
            pool.affine_select(out=ident[:, :], in_=ident[:, :], compare_op=ALU.not_equal, fill=1.0,
                               base=0, pattern=[[-1, P]], channel_multiplier=1).then_inc(consts, 1)
            pool.affine_select(out=sel[:, :], in_=sel[:, :], compare_op=ALU.not_equal, fill=1.0,
                               base=-(DE + 1), pattern=[[0, 1]], channel_multiplier=1).then_inc(consts, 1)
            pool.memset(zeros[:, :], 0.0).then_inc(consts, 1)
            pool.memset(ones_col[:, :], 1.0).then_inc(consts, 1)
            pool.memset(erow[:, :, :], 1.0).then_inc(consts, 1)

            for r in range(3):
                pool.wait_ge(table_out, 16 * (r + 1))
                with pool.Fori(0, HALF) as i:
                    for k in range(2):
                        pool.wait_ge(idx_ready, 2 * i + k + 1 + r * C)
                        pool.wait_ge(msg_ready, 2 * i + k + 1 + r * C)
                        pool.sem_inc(pool_turn, 1)
                        pool.indirect_dma_start(
                            out=gath[:, k, :], out_offset=None, in_=table[:, :],
                            in_offset=bass.IndirectOffsetOnAxis(ap=slotI[:, k, :], axis=0)).then_inc(gath_in[k], 16)

        @block.scalar
        def _(act):
            for r in range(4):
                act.wait_ge(sum_done, r + 1)
                dstT = edgeT if r == 0 else sumT
                rows = DX if r == 0 else P
                for b in range(NB):
                    lo, hi = b * BANK, min(NP, (b + 1) * BANK)
                    act.activation(dstT[0:rows, lo:hi], acc[0:rows, lo:hi], ACT.Copy).then_inc(sum_copied, 1)
                if r == 0:
                    act.wait_ge(ln_var, 1)
                    act.activation(std[:, :], std[:, :], ACT.Sqrt).then_inc(ln_std, 1)
                    act.wait_ge(deg_safe, 1)
                    act.activation(degpos[:, :], deg[:, :], ACT.Sqrt).then_inc(deg_sqrt, 1)
                if r == 1:
                    act.wait_ge(ln_var, 2)
                    act.activation(std[:, :], std[:, :], ACT.Sqrt).then_inc(ln_std, 1)

        @block.tensor
        def _(pe):
            pe.wait_ge(consts, 6)
            pe.wait_ge(lists_f, 3)
            for f in range(3):
                for k in range(K):
                    mm = pe.transpose(acc[:, f * BANK + k * PL:f * BANK + (k + 1) * PL],
                                      listF[0:PL, f, k * P:(k + 1) * P], ident[0:PL, 0:PL])
            mm.then_inc(lists_t, 1)
            for r in range(4):
                if r == 0:
                    pe.wait_ge(meta_ready, 1)
                elif r == 1:
                    pe.wait_ge(sum_copied, NB)
                else:
                    pe.wait_ge(z_ready, r)
                rows = DX if r == 0 else P
                for b in range(NB):
                    lo, hi = b * BANK, min(NP, (b + 1) * BANK)
                    pe.matmul(acc[0:rows, lo:hi], zeros[:, 0:rows], zeros[:, 0:hi - lo], start=True, stop=False,
                              skip_group_check=True)
                with pe.Fori(0, HALF) as i:
                    for k in range(2):
                        if r == 0:
                            pe.wait_ge(erow_in[k], i * 16 + 16)
                            pe.wait_ge(ew_ready, 2 * i + k + 1)
                            lhs = erow[:, k, :]
                        else:
                            pe.wait_ge(msg_ready, 2 * i + k + 1 + (r - 1) * C + 2)
                            lhs = msg[:, k, :]
                        pe.wait_ge(oh_ready, 2 * i + k + 1 + r * C)
                        for b in range(NB):
                            lo, hi = b * BANK, min(NP, (b + 1) * BANK)
                            mm = pe.matmul(acc[0:rows, lo:hi], lhs, onehot[:, k, lo:hi], start=False, stop=False,
                                           skip_group_check=True)
                        mm.then_inc(chunk_done, 1)
                if r >= 2:
                    for t in range(T):
                        mm = pe.matmul(acc[:, t * P:(t + 1) * P], z_sb[:, t, :], ident[:, :], start=False,
                                       stop=False, skip_group_check=True)
                else:
                    mm = pe.matmul(acc[0:rows, NP - P:NP], zeros[:, 0:rows], zeros[:, 0:P], start=False, stop=False,
                                   skip_group_check=True)
                mm.then_inc(sum_done, 1)
                pe.wait_ge(sum_copied, (r + 1) * NB)
                if r == 0:
                    for t in range(T):
                        mm = pe.matmul(misc[:, t:t + 1], edgeT[0:DX, t * P:(t + 1) * P], sel[0:DX, :],
                                       start=True, stop=True)
                    mm.then_inc(deg_done, 1)
                    continue
                pe.wait_ge(weights_in, 16 * 8)
                pe.wait_ge(zeroed, 1)
                w = (wl, w1, w2)[r - 1]
                for t in range(T):
                    cols = slice(t * P, (t + 1) * P)
                    mm = pe.matmul(acc[:, cols], sumT[:, cols], w[:, :], start=True, stop=(r > 1))
                    if r == 1:
                        mm = pe.matmul(acc[:, cols], edgeT[0:DX, cols], we[0:DX, :], start=False, stop=True)
                mm.then_inc(proj_done, 1)

        @block.vector
        def _(dve):
            chain = [0]

            def link(ins):
                chain[0] += 1
                ins.then_inc(dve_chain, 1)
                dve.wait_ge(dve_chain, chain[0])

            def wide(col):
                return col.unsqueeze(2).broadcast_to([P, T, D])

            def layer_norm_relu(r):
                for t in range(T):
                    last = dve.bn_stats(stats[:, t, :], x_sb[:, t, :])
                link(last)
                for t in range(T):
                    last = dve.bn_aggr(mv[:, t, :], stats[:, t, :])
                link(last)
                dve.tensor_scalar(std[:, :], mv[:, :, 1], EPS, None, ALU.add).then_inc(ln_var, 1)
                dve.wait_ge(ln_std, r + 1)
                link(dve.reciprocal(rstd[:, :], std[:, :]))
                link(dve.tensor_tensor(z_sb[:, :, :], x_sb[:, :, :], wide(mv[:, :, 0]), ALU.subtract))
                link(dve.tensor_tensor(z_sb[:, :, :], z_sb[:, :, :], wide(rstd[:, :]), ALU.mult))

            dve.wait_ge(pads_set, 5)
            dve.wait_ge(lists_in, 16 * 6)
            for f in range(2):
                dve.tensor_copy(listF[:, f, :], listI[:, f, :]).then_inc(lists_f, 1)
            dve.nop().then_inc(lists_f, 1)
            dve.wait_ge(lists_t, 1)
            for f in range(3):
                last = dve.tensor_copy(meta[:, :, f].rearrange("p (l k) -> p l k", k=K),
                                       acc[:, f * BANK:f * BANK + K * PL].rearrange("p (k l) -> p l k", k=K))
            last.then_inc(meta_ready, 1)
            dve.wait_ge(meta_ready, 1)
            dve.sem_inc(chunk_done, 2)
            dve.wait_ge(consts, 6)

            def one_hot(r, i, k):
                dve.tensor_scalar(onehot[:, k, :], iota_n[:, :], slotF[:, k, 0:1], None,
                                  ALU.is_equal).then_inc(oh_ready, 1)

            with dve.Fori(0, HALF) as i:
                for k in range(2):
                    dve.wait_ge(chunk_done, 2 * i + k + 1)
                    dve.tensor_copy(slotF[:, k, :], meta[:, bass.ds(2 * i + k, 1), :].rearrange("p a f -> p (a f)")).then_inc(ew_ready, 1)
                    dve.tensor_copy(erow[:, k, DE + 1:DX], meta[:, bass.ds(2 * i + k, 1), 2:3].rearrange("p a f -> p (a f)"))
                    dve.wait_ge(ew_ready, 2 * i + k + 1)
                    one_hot(0, i, k)

            dve.wait_ge(x_in, 32)
            layer_norm_relu(0)
            dve.tensor_scalar(z_sb[:, :, :], z_sb[:, :, :], 0.0, None, ALU.max).then_inc(z_ready, 1)
            dve.wait_ge(weights_in, 16 * 8)
            dve.tensor_tensor(we[DE:DE + 1, :], we[DE:DE + 1, :], be[DE:DE + 1, :], ALU.add).then_inc(zeroed, 1)
            dve.wait_ge(deg_done, 1)
            link(dve.tensor_scalar(deg[:, :], misc[:, 0:T], 1.0, None, ALU.add))
            link(dve.tensor_scalar(dinv[:, :], deg[:, :], 0.0, None, ALU.is_gt))
            dve.tensor_scalar(deg[:, :], deg[:, :], 1e-30, None, ALU.max).then_inc(deg_safe, 1)
            dve.wait_ge(deg_sqrt, 1)
            link(dve.reciprocal(degpos[:, :], degpos[:, :]))
            link(dve.tensor_tensor(dinv[:, :], dinv[:, :], degpos[:, :], ALU.mult))

            dve.sem_inc(msg_ready, 2)
            for r in range(3):
                dve.wait_ge(chunk_done, (r + 1) * C + 2)
                with dve.Fori(0, HALF) as i:
                    for k in range(2):
                        n = 2 * i + k + 1
                        dve.wait_ge(chunk_done, n + (r + 1) * C)
                        dve.tensor_copy(slotF[:, k, :], meta[:, bass.ds(2 * i + k, 1), :].rearrange("p a f -> p (a f)")).then_inc(ew_ready, 1)
                        dve.tensor_copy(slotI[:, k, :], meta[:, bass.ds(2 * i + k, 1), 1:2].rearrange("p a f -> p (a f)")).then_inc(idx_ready, 1)
                        dve.wait_ge(ew_ready, n + (r + 1) * C)
                        one_hot(r + 1, i, k)
                        dve.wait_ge(gath_in[k], i * 16 + 16 + r * HALF * 16)
                        dve.tensor_scalar(msg[:, k, :], gath[:, k, :], ones_col[:, :] if r == 0 else slotF[:, k, 2:3],
                                          None, ALU.mult).then_inc(msg_ready, 1)
                dve.wait_ge(proj_done, r + 1)
                proj = acc[:, 0:NP].rearrange("p (t f) -> p t f", f=D)
                if r == 0:
                    link(dve.scalar_tensor_tensor(out=x_sb[:, :, :], in0=proj, scalar=0.0, in1=x_sb[:, :, :],
                                                  op0=ALU.max, op1=ALU.add))
                    layer_norm_relu(1)
                    link(dve.tensor_scalar(z_sb[:, :, :], z_sb[:, :, :], 0.0, None, ALU.max))
                    dve.tensor_tensor(z_sb[:, :, :], z_sb[:, :, :], wide(dinv[:, :]), ALU.mult).then_inc(z_ready, 1)
                    continue
                bias = (b1s, b2s)[r - 1][:, :].unsqueeze(1).broadcast_to([P, T, D])
                link(dve.tensor_tensor(z_sb[:, :, :], proj, wide(dinv[:, :]), ALU.mult))
                link(dve.tensor_tensor(z_sb[:, :, :], z_sb[:, :, :], bias, ALU.add))
                if r == 1:
                    link(dve.tensor_scalar(z_sb[:, :, :], z_sb[:, :, :], 0.0, None, ALU.max))
                    dve.tensor_tensor(z_sb[:, :, :], z_sb[:, :, :], wide(dinv[:, :]), ALU.mult).then_inc(z_ready, 1)
                else:
                    dve.tensor_tensor(z_sb[:, :, :], z_sb[:, :, :], x_sb[:, :, :], ALU.add).then_inc(out_ready, 1)


_INS = ['x', 'src', 'dst', 'edge_attr_64', 'edge_weight', 'L0_gnn_W_lin', 'L0_gnn_b_lin', 'L0_gnn_W_edge',
        'L0_gnn_b_edge', 'L1_gnn_W1', 'L1_gnn_b1', 'L1_gnn_W2', 'L1_gnn_b2']


def kernel(**inputs):
    import numpy as _np
    import concourse.bacc as _bacc
    from concourse import mybir as _mybir
    from concourse.bass_utils import run_bass_kernel_spmd as _run

    nc = _bacc.Bacc("TRN2", target_bir_lowering=False, num_devices=1)
    arrays, args = {}, []
    for name in _INS:
        a = _np.ascontiguousarray(inputs[name])
        arrays[f"in_{name}_dram"] = a
        args.append(nc.dram_tensor(f"in_{name}_dram", a.shape, _mybir.dt.from_np(a.dtype), kind="ExternalInput").ap())
    out = nc.dram_tensor("out_dram", inputs["x"].shape, _mybir.dt.float32, kind="ExternalOutput").ap()
    build_graph_layers(nc, *args, out)
    r = _run(nc, [arrays], core_ids=[0])
    return r.results[0]["out_dram"]
```

```python
from contextlib import ExitStack

import concourse.bass as bass
from concourse import mybir

F32 = mybir.dt.float32
BF16 = mybir.dt.bfloat16
I32 = mybir.dt.int32
ALU = mybir.AluOpType
ACT = mybir.ActivationFunctionType

P = 128
BANK = 512


def build_graph_layers(nc, x, src, dst, edge_attr, edge_weight, W_lin, b_lin, W_edge, b_edge,
                       W1, b1, W2, b2, out):
    N, D = x.shape
    E, DE = edge_attr.shape
    T = -(-N // P)
    NP = T * P
    NR = N - (T - 1) * P
    C = -(-E // P)
    ER = E - (C - 1) * P
    K = 4
    PL = C // K
    LROW = K * P
    LR = E - (PL - 1) * LROW
    DX = DE + 2
    NB = -(-NP // BANK)
    EPS = 1e-5
    assert C % K == 0 and PL <= P and D == P and DX <= P

    TC = T + 1
    MX = 6
    REC = DE + MX
    STG = 2
    NSTG = 4
    UNIT = STG * NSTG
    UNITS = C // UNIT
    assert C % UNIT == 0 and T % 2 == 1

    table = nc.dram_tensor("node_table", [NP, D], F32, kind="Internal").ap()
    records = nc.dram_tensor("records", [T * P * TC, REC], F32, kind="Internal").ap()
    wmat = nc.dram_tensor("wmat", [NP, NP], F32, kind="Internal").ap()

    with ExitStack() as ctx:
        def sb(name, shape, dt=F32):
            return ctx.enter_context(nc.sbuf_tensor(name, shape, dt))

        def sem(name):
            return ctx.enter_context(nc.semaphore(name))

        def psum(name, shape, dt=F32):
            return ctx.enter_context(nc.psum_tensor(name, shape, dt))

        x_sb = sb("x_sb", [P, T, D])
        z_sb = sb("z_sb", [P, T, D])
        sumT = sb("sumT", [P, NP])
        edge_buf = sb("edge_buf", [P, 2 * T * DX])
        edgeT = edge_buf[:, 0:NP]
        edge_row = edge_buf[:, :].rearrange("p (a t d) -> p a t d", a=2, t=T)
        arena = sb("arena", [P, 4 * NP])
        rows = arena[:, :].rearrange("p (a m n) -> p a m n", a=2, m=2)
        wslot = arena[:, :].rearrange("p (k n) -> p k n", k=4)
        iota_n = arena[:, 0:NP]
        onehot = arena[:, NP:3 * NP].rearrange("p (k n) -> p k n", k=2)
        arena_b = arena[:, :].bitcast(BF16)
        oh_src = arena_b[:, 0:T * C].rearrange("p (j c) -> p j c", j=T)
        oh_dst = arena_b[:, T * C:2 * T * C]
        rec = sb("rec", [P, 2, TC, REC])
        stage = sb("stage", [P, NSTG, STG, REC])
        metaX = sb("metaX", [P, C, MX])
        metaP = sb("metaP", [P, 3, C])
        edge_acc = sb("edge_acc", [P, T, DX])
        last_row = sb("last_row", [P, D])
        ohd = sb("ohd", [P, 4, P])
        ohs = sb("ohs", [P, 4, P])
        ohw = sb("ohw", [P, 4, P])
        hslot = sb("hslot", [P, 4, D])
        iotaF = sb("iotaF", [P, P])
        iotaD = sb("iotaD", [P, P])
        pcol = sb("pcol", [P, 1])
        ident = sb("ident", [P, P])
        identB = sb("identB", [P, P], BF16)
        triB = sb("triB", [P, P], BF16)
        pick = sb("pick", [P, 2 * T - 1], BF16)
        spread = sb("spread", [T, T, P], BF16)
        zeros = sb("zeros", [P, BANK])
        ones_col = sb("ones_col", [P, 1])
        listI = sb("listI", [P, 2, LROW + 1], I32)
        listF = sb("listF", [P, 3, LROW])
        ti = sb("ti", [P, 3, C], I32)
        tf = sb("tf", [P, 6, C])
        shiB = sb("shiB", [P, C], BF16)
        dhiB = sb("dhiB", [P, C], BF16)
        cumB = sb("cumB", [T, C], BF16)
        before = sb("before", [P, C])
        bad = sb("bad", [P, 4])
        cnt = sb("cnt", [P, 5 * T])
        rowsum = sb("rowsum", [T, 1])
        upto = sb("upto", [T, T])
        unitF = sb("unitF", [1, T])
        unitI = sb("unitI", [1, T + 1], I32)
        flagI = sb("flagI", [1, 1], I32)
        slotF = sb("slotF", [P, 2, 3])
        slotI = sb("slotI", [P, 2, 1], I32)
        erow = sb("erow", [P, 2, DX])
        gath = sb("gath", [P, 2, D])
        msg = sb("msg", [P, 2, D])
        wl = sb("wl", [P, D])
        we = sb("we", [P, D])
        be = sb("be", [P, D])
        w1 = sb("w1", [P, D])
        w2 = sb("w2", [P, D])
        b1s = sb("b1s", [P, D])
        b2s = sb("b2s", [P, D])
        stats = sb("stats", [P, T, 6])
        mv = sb("mv", [P, T, 2])
        std = sb("std", [P, T])
        rstd = sb("rstd", [P, T])
        deg = sb("deg", [P, T])
        degpos = sb("degpos", [P, T])
        dinv = sb("dinv", [P, T])
        sel = sb("sel", [P, 1])
        acc = psum("acc", [P, 8 * BANK])
        work = [acc[:, (6 + q) * BANK:(7 + q) * BANK] for q in range(2)]

        x_in = sem("x_in")
        lists_in = sem("lists_in")
        weights_in = sem("weights_in")
        pads_set = sem("pads_set")
        pool_consts = sem("pool_consts")
        consts = sem("consts")
        zeros_out = sem("zeros_out")
        bias_sum = sem("bias_sum")
        lists_f = sem("lists_f")
        lists_t = sem("lists_t")
        hi_ready = sem("hi_ready")
        oh_src_ready = sem("oh_src_ready")
        oh_dst_ready = sem("oh_dst_ready")
        tot_done = sem("tot_done")
        cum_ready = sem("cum_ready")
        rank_done = sem("rank_done")
        rank_taken = sem("rank_taken")
        pairs_done = sem("pairs_done")
        pairs_copied = sem("pairs_copied")
        count_done = sem("count_done")
        bad_ready = sem("bad_ready")
        rowsum_ready = sem("rowsum_ready")
        cum_done = sem("cum_done")
        bad_done = sem("bad_done")
        flag_ready = sem("flag_ready")
        ln_var = sem("ln_var")
        ln_std = sem("ln_std")
        z_ready = sem("z_ready")
        table_out = sem("table_out")
        gen_consts = sem("gen_consts")
        erow_in = [sem(f"erow_in{k}") for k in range(2)]
        ew_ready = sem("ew_ready")
        idx_ready = sem("idx_ready")
        gath_in = [sem(f"gath_in{k}") for k in range(2)]
        msg_ready = sem("msg_ready")
        oh_ready = sem("oh_ready")
        chunk_done = sem("chunk_done")
        stage_in = [sem(f"stage_in{k}") for k in range(NSTG)]
        scattered = [sem(f"scattered{k}") for k in range(NSTG)]
        rec_in = [sem(f"rec_in{k}") for k in range(2)]
        ohd_ready = sem("ohd_ready")
        ohw_ready = sem("ohw_ready")
        built = sem("built")
        evac = sem("evac")
        diag_taken = sem("diag_taken")
        edge_added = sem("edge_added")
        row_ready = sem("row_ready")
        h_ready = sem("h_ready")
        row_summed = sem("row_summed")
        last_added = sem("last_added")
        last_taken = sem("last_taken")
        w_out = [sem(f"w_out{k}") for k in range(2)]
        w_stored = sem("w_stored")
        edge_t = sem("edge_t")
        w_in = [sem(f"w_in{k}") for k in range(4)]
        w_used = sem("w_used")
        sum_done = sem("sum_done")
        sum_copied = sem("sum_copied")
        deg_done = sem("deg_done")
        proj_done = sem("proj_done")
        deg_safe = sem("deg_safe")
        deg_sqrt = sem("deg_sqrt")
        out_ready = sem("out_ready")
        out_done = sem("out_done")
        dve_chain = sem("dve_chain")
        pool_turn = sem("pool_turn")

        HALF = C // 2
        banks = [(b * BANK, min(NP, (b + 1) * BANK)) for b in range(NB)]
        block = ctx.enter_context(nc.Block())

        def sorted_fits(eng):
            eng.wait_ge(flag_ready, 1)
            return eng.value_load(flagI[0:1, 0:1], min_val=0, max_val=1)

        def build_tiles(eng, body):
            for par in range(2):
                body(0, par)
            with eng.Fori(1, T // 2) as tt:
                for par in range(2):
                    body(tt, par)
            body(T // 2, 0)

        @block.sync
        def _(sp):
            full = (PL - 1) * LROW
            sp.wait_ge(pads_set, 3)
            for f, a in ((1, dst), (0, src)):
                sp.dma_start(listI[0:PL - 1, f, 0:LROW], a[0:full].rearrange("(p n) -> p n", n=LROW)).then_inc(lists_in, 16)
                sp.dma_start(listI[PL - 1:PL, f, 0:LR], a[full:E].rearrange("(p n) -> p n", p=1)).then_inc(lists_in, 16)
            sp.dma_start(listI[0:PL - 1, 1, LROW:LROW + 1],
                         dst[LROW:full + 1:LROW].rearrange("(p n) -> p n", n=1),
                         allow_slow_non_contiguous=True).then_inc(lists_in, 16)
            sp.dma_start(listF[0:PL - 1, 2, :], edge_weight[0:full].rearrange("(p n) -> p n", n=LROW)).then_inc(lists_in, 16)
            sp.dma_start(listF[PL - 1:PL, 2, 0:LR], edge_weight[full:E].rearrange("(p n) -> p n", p=1)).then_inc(lists_in, 16)
            sp.dma_start(x_sb[:, 0:T - 1, :], x[0:(T - 1) * P, :].rearrange("(t p) f -> p t f", p=P)).then_inc(x_in, 16)
            sp.wait_ge(pads_set, 6)
            sp.dma_start(x_sb[0:NR, T - 1, :], x[(T - 1) * P:N, :]).then_inc(x_in, 16)
            for t in range(T):
                sp.dma_start(records[t * P * TC:(t + 1) * P * TC, :].rearrange("(p j) r -> p j r", p=P),
                             rec[:, 0, :, :]).then_inc(zeros_out, 16)
            sp.dma_start(wl[:, :], W_lin).then_inc(weights_in, 16)
            sp.dma_start(w1[:, :], W1).then_inc(weights_in, 16)
            sp.dma_start(w2[:, :], W2).then_inc(weights_in, 16)
            sp.dma_start(we[0:DE, :], W_edge).then_inc(weights_in, 16)
            sp.dma_start(we[DE:DE + 1, :], b_lin.rearrange("(a d) -> a d", a=1)).then_inc(weights_in, 16)
            sp.dma_start(be[DE:DE + 1, :], b_edge.rearrange("(a d) -> a d", a=1)).then_inc(weights_in, 16)
            sp.dma_start(b1s[:, :], b1.rearrange("(a d) -> a d", a=1).broadcast_to([P, D])).then_inc(weights_in, 16)
            sp.dma_start(b2s[:, :], b2.rearrange("(a d) -> a d", a=1).broadcast_to([P, D])).then_inc(weights_in, 16)

            fast = sorted_fits(sp)
            with sp.If(fast):
                def stage_load(unit, k, last=False):
                    row = unit * (UNIT * P) + k * (STG * P)
                    if last:
                        at = (C - STG) * P
                        sp.dma_start(stage[:, k, 0, 0:DE], edge_attr[at:at + P, :]).then_inc(stage_in[k], 16)
                        sp.dma_start(stage[0:ER, k, 1, 0:DE], edge_attr[at + P:E, :]).then_inc(stage_in[k], 16)
                    else:
                        sp.dma_start(stage[:, k, :, 0:DE],
                                     edge_attr[bass.ds(row, STG * P), :].rearrange("(c p) f -> p c f", p=P)).then_inc(stage_in[k], 16)
                    sp.dma_start(stage[:, k, :, DE:REC],
                                 metaX[:, bass.ds(unit * UNIT + k * STG, STG), :]).then_inc(stage_in[k], 16)

                for k in range(NSTG):
                    stage_load(0, k)
                def next_units(first, end):
                    with sp.If(first < end):
                        with sp.Fori(first, end) as n:
                            for k in range(NSTG):
                                sp.wait_ge(scattered[k], n * (16 * STG) + 16 * STG)
                                stage_load(n + 1, k)

                def unit(t):
                    return sp.value_load(unitI[0:1, bass.ds(t, 1)], min_val=0, max_val=UNITS - 2)

                def load_records(t, par):
                    sp.wait_ge(edge_added, t + 1)
                    sp.dma_start(rec[:, par, :, :], records[bass.ds(t * (P * TC), P * TC), :]
                                 .rearrange("(p j) r -> p j r", p=P)).then_inc(rec_in[par], 16)

                with sp.Fori(0, (T - 3) // 2) as tt:
                    for par in range(2):
                        next_units(unit(tt * 2 + par), unit(tt * 2 + (par + 1)))
                        load_records(tt * 2 + par, par)
                next_units(unit(T - 3), unit(T - 2))
                load_records(T - 3, (T - 3) % 2)
                next_units(unit(T - 2), UNITS - 2)
                for k in range(NSTG):
                    sp.wait_ge(scattered[k], (UNITS - 1) * 16 * STG)
                    stage_load(UNITS - 1, k, last=(k == NSTG - 1))
                for k in range(NSTG):
                    sp.wait_ge(scattered[k], UNITS * 16 * STG)
                for t in (T - 2, T - 1):
                    load_records(t, t % 2)

                sp.wait_ge(w_stored, 1)
                sp.wait_ge(sum_done, 1)
                for r in range(2):
                    if r:
                        sp.wait_ge(w_used, T + 4)
                    with sp.Fori(0, T // 4) as q:
                        for k in range(4):
                            sp.wait_ge(w_used, q * 4 + (k + 1 + r * T))
                            sp.dma_start(wslot[:, k, :], wmat[bass.ds(q * (4 * P) + k * P, P), :]).then_inc(w_in[k], 16)
                    sp.wait_ge(w_used, (r + 1) * T)
                    sp.dma_start(wslot[:, 0, :], wmat[(T - 1) * P:T * P, :]).then_inc(w_in[0], 16)
            with sp.Else():
                sp.wait_ge(zeros_out, 16 * T)
                sp.wait_ge(gen_consts, 2)
                with sp.Fori(0, HALF - 1) as i:
                    for k in range(2):
                        sp.wait_ge(chunk_done, 2 * i + k + 1)
                        sp.dma_start(erow[:, k, 0:DE], edge_attr[bass.ds(i * (2 * P) + k * P, P), :]).then_inc(erow_in[k], 16)
                sp.wait_ge(chunk_done, C - 1)
                sp.dma_start(erow[:, 0, 0:DE], edge_attr[(C - 2) * P:(C - 1) * P, :]).then_inc(erow_in[0], 16)
                sp.wait_ge(chunk_done, C)
                sp.dma_start(erow[0:ER, 1, 0:DE], edge_attr[(C - 1) * P:E, :]).then_inc(erow_in[1], 16)
                for r in range(3):
                    sp.wait_ge(z_ready, r + 1)
                    if r:
                        sp.wait_ge(sum_done, r + 1)
                    sp.dma_start(table.rearrange("(t p) f -> p t f", p=P), z_sb[:, :, :]).then_inc(table_out, 16)
                    sp.wait_ge(table_out, 16 * (r + 1))
            sp.wait_ge(out_ready, 1)
            sp.dma_start(out[0:(T - 1) * P, :].rearrange("(t p) f -> p t f", p=P), z_sb[:, 0:T - 1, :]).then_inc(out_done, 16)
            sp.dma_start(out[(T - 1) * P:N, :], z_sb[0:NR, T - 1, :]).then_inc(out_done, 16)
            sp.wait_ge(out_done, 32)

        @block.gpsimd
        def _(pool):
            pool.memset(listI[:, 0, :], -1).then_inc(pads_set, 1)
            pool.memset(listI[:, 1, :], N - 1).then_inc(pads_set, 1)
            pool.memset(listF[:, 2, :], 0.0).then_inc(pads_set, 1)
            pool.iota(iotaF[:, :], [[1, P]], base=0, channel_multiplier=0,
                      allow_small_or_imprecise_dtypes=True).then_inc(pool_consts, 1)
            pool.iota(pcol[:, :], [[0, 1]], base=0, channel_multiplier=1,
                      allow_small_or_imprecise_dtypes=True).then_inc(pool_consts, 1)
            pool.memset(rec[:, 0, :, :], 0.0).then_inc(pads_set, 1)
            pool.memset(x_sb[:, T - 1, :], 0.0).then_inc(pads_set, 1)
            pool.memset(we[:, :], 0.0).then_inc(pads_set, 1)
            pool.memset(zeros[:, :], 0.0).then_inc(pool_consts, 1)
            pool.memset(ones_col[:, :], 1.0).then_inc(pool_consts, 1)
            pool.memset(metaX[:, :, :], 1.0).then_inc(pool_consts, 1)
            pool.memset(edge_acc[:, :, :], 0.0).then_inc(pool_consts, 1)
            fast = sorted_fits(pool)
            with pool.If(fast):
                pool.wait_ge(zeros_out, 16 * T)

                def scatter(k, c, n=P):
                    pool.indirect_dma_start(
                        out=records[:, :], out_offset=bass.IndirectOffsetOnAxis(
                            ap=stage[0:n, k, c, DE + 4:DE + 5].bitcast(I32), axis=0),
                        in_=stage[0:n, k, c, :], in_offset=None).then_inc(scattered[k], 16)

                with pool.Fori(0, UNITS - 1) as n:
                    for k in range(NSTG):
                        pool.wait_ge(stage_in[k], n * 32 + 32)
                        pool.sem_inc(pool_turn, 1)
                        for c in range(STG):
                            scatter(k, c)
                for k in range(NSTG):
                    pool.wait_ge(stage_in[k], UNITS * 32 + (16 if k == NSTG - 1 else 0))
                    for c in range(STG):
                        scatter(k, c, ER if k == NSTG - 1 and c == STG - 1 else P)
            with pool.Else():
                pool.iota(iota_n, [[1, NP]], base=0, channel_multiplier=0,
                          allow_small_or_imprecise_dtypes=True).then_inc(gen_consts, 1)
                pool.memset(erow[:, :, :], 1.0).then_inc(gen_consts, 1)
                for r in range(3):
                    pool.wait_ge(table_out, 16 * (r + 1))
                    with pool.Fori(0, HALF) as i:
                        for k in range(2):
                            pool.wait_ge(idx_ready, 2 * i + k + 1 + r * C)
                            pool.wait_ge(msg_ready, 2 * i + k + 1 + r * C)
                            pool.sem_inc(pool_turn, 1)
                            pool.indirect_dma_start(
                                out=gath[:, k, :], out_offset=None, in_=table[:, :],
                                in_offset=bass.IndirectOffsetOnAxis(ap=slotI[:, k, :], axis=0)).then_inc(gath_in[k], 16)

        @block.scalar
        def _(act):
            act.wait_ge(ln_var, 1)
            act.activation(std[:, :], std[:, :], ACT.Sqrt).then_inc(ln_std, 1)

            def copy_sums(done, dstT, n):
                act.wait_ge(sum_done, done)
                for lo, hi in banks:
                    act.activation(dstT[0:n, lo:hi], acc[0:n, lo:hi], ACT.Copy).then_inc(sum_copied, 1)

            fast = sorted_fits(act)
            with act.If(fast):
                def weigh(tt, u):
                    s, j = u % 4, u % TC
                    act.wait_ge(ohd_ready, tt * (2 * TC) + u + 1)
                    act.activation(ohw[:, s, :], ohs[:, s, :], ACT.Copy,
                                   scale=rec[:, (u // TC) % 2, j, DE + 1:DE + 2]).then_inc(ohw_ready, 1)

                AHEAD = 2

                def take_last(t):
                    act.wait_ge(last_added, t)
                    act.activation(last_row[:, :], work[0][:, 3 * P:4 * P], ACT.Copy).then_inc(last_taken, 1)

                def store_row(tt, par):
                    act.wait_ge(row_ready, tt * 2 + (par + 1))
                    at = wmat[bass.ds(tt * (2 * P) + par * P, P), :]
                    act.dma_start(at, rows[:, par, 1, :]).then_inc(w_out[par], 16)

                def tile(tt, par):
                    t = tt * 2 + par
                    first = isinstance(tt, int) and tt == 0 and par == 0
                    before_ = (tt, 0) if par else (tt - 1, 1)
                    for j in range(TC):
                        u = par * TC + j
                        if not (isinstance(tt, int) and tt == T // 2 and j + AHEAD >= TC):
                            weigh(tt, u + AHEAD)
                        if j == 0:
                            act.wait_ge(row_summed, t + 1)
                            act.wait_ge(edge_added, t + 1)
                        if j == 1:
                            act.activation(hslot[:, par, :], z_sb[:, bass.ds(t, 1), :].rearrange("p a f -> p (a f)"),
                                           ACT.Copy).then_inc(h_ready, 1)
                        if j == 3 and not first:
                            store_row(*before_)
                        if j == TC - 1:
                            if not first:
                                act.wait_ge(w_out[1 - par], before_[0] * 16 + 16)
                            continue
                        act.wait_ge(built, tt * (2 * TC) + (u + 5))
                        if j == 4 and not first:
                            take_last(tt * 2 + par)
                        act.activation(rows[:, par, :, j * P:(j + 1) * P],
                                       work[j % 2][:, 0:2 * P].rearrange("p (m n) -> p m n", m=2), ACT.Copy)
                        act.activation(edge_row[:, par, j, :], work[j % 2][:, 2 * P:2 * P + DX], ACT.Copy).then_inc(evac, 1)

                act.wait_ge(z_ready, 1)
                for u in range(AHEAD):
                    weigh(0, u)
                build_tiles(act, tile)
                store_row(T // 2, 0)
                act.wait_ge(row_summed, T + 2)
                take_last(T)
                copy_g0 = 6
                act.wait_ge(sum_done, 1)
                for lo, hi in banks[:copy_g0]:
                    act.activation(sumT[:, lo:hi], acc[:, lo:hi], ACT.Copy).then_inc(sum_copied, 1)
                act.wait_ge(w_out[0], 16 * (T // 2 + 1))
                act.sem_inc(w_stored, 1)
                for g in range(-(-T // 4)):
                    n = min(4, T - 4 * g)
                    act.wait_ge(edge_t, g + 1)
                    act.activation(edgeT[0:DX, g * BANK:g * BANK + n * P], work[g % 2][0:DX, 0:n * P],
                                   ACT.Copy).then_inc(sum_copied, 1)
                act.sem_inc(sum_copied, 2 * NB - copy_g0 - -(-T // 4))
            with act.Else():
                copy_sums(1, edgeT, DX)
                copy_sums(2, sumT, P)
            act.wait_ge(deg_safe, 1)
            act.activation(degpos[:, :], deg[:, :], ACT.Sqrt).then_inc(deg_sqrt, 1)
            act.wait_ge(ln_var, 2)
            act.activation(std[:, :], std[:, :], ACT.Sqrt).then_inc(ln_std, 1)
            for r in range(2):
                with act.If(fast):
                    act.wait_ge(z_ready, r + 2)
                    if r:
                        act.wait_ge(w_used, T + 4)

                    def copy_z(t, k, n):
                        act.wait_ge(w_used, n)
                        act.activation(hslot[:, k, :], z_sb[:, bass.ds(t, 1), :].rearrange("p a f -> p (a f)"),
                                       ACT.Copy).then_inc(h_ready, 1)

                    with act.Fori(0, T // 4) as q:
                        for k in range(4):
                            copy_z(q * 4 + k, k, q * 4 + (k + 1 + r * T))
                    copy_z(T - 1, 0, (r + 1) * T)
                copy_sums(3 + r, sumT, P)

        @block.tensor
        def _(pe):
            pe.wait_ge(consts, 1)
            pe.wait_ge(pool_consts, 6)
            pe.wait_ge(lists_f, 2)
            for f in range(3):
                for k in range(K):
                    mm = pe.transpose(acc[:, f * BANK + k * PL:f * BANK + (k + 1) * PL],
                                      listF[0:PL, f, k * P:(k + 1) * P], ident[0:PL, 0:PL])
            mm.then_inc(lists_t, 1)
            pe.wait_ge(oh_src_ready, 1)
            tot = acc[0:T, 7 * BANK:7 * BANK + C]
            for j in range(T):
                mm = pe.matmul(tot, pick[:, T - 1 - j:2 * T - 1 - j], oh_src[:, j, :], start=(j == 0), stop=(j == T - 1))
            mm.then_inc(tot_done, 1)
            pe.wait_ge(cum_ready, 1)
            for j in range(T):
                if j >= 4:
                    pe.wait_ge(rank_taken, j - 3)
                o = acc[:, (j % 4) * BANK:(j % 4) * BANK + C]
                pe.matmul(o, triB[:, :], oh_src[:, j, :], start=True, stop=False)
                pe.matmul(o, spread[:, j, :], cumB[:, :], start=False, stop=True).then_inc(rank_done, 1)
            pe.wait_ge(oh_dst_ready, 1)
            G = 5
            pairs = acc[0:G * T, 5 * BANK:5 * BANK + G * T].rearrange("p (c j) -> p c j", c=G)
            src_by_chunk = oh_src.rearrange("p j c -> p c j")
            pe.matmul(pairs, oh_dst[:, 0:G * T], src_by_chunk[:, 0:G, :], start=True, stop=False, skip_group_check=True)
            with pe.Fori(1, C // G) as q:
                pe.matmul(pairs, oh_dst[:, bass.ds(q * (G * T), G * T)], src_by_chunk[:, bass.ds(q * G, G), :],
                          start=False, stop=False, skip_group_check=True)
            mm = pe.matmul(pairs[0:T, 0, :], oh_dst[:, (C - 1) * T:C * T], src_by_chunk[:, C - 1, :],
                           start=False, stop=True, skip_group_check=True)
            mm.then_inc(pairs_done, 1)
            pe.wait_ge(pairs_copied, 1)
            for g in range(G):
                mm = pe.matmul(acc[0:T, 4 * BANK:4 * BANK + T], ident[0:G * T, g * T:(g + 1) * T],
                               cnt[0:G * T, g * T:(g + 1) * T], start=(g == 0), stop=(g == G - 1))
            mm.then_inc(count_done, 1)
            pe.wait_ge(rowsum_ready, 1)
            pe.matmul(acc[0:1, 6 * BANK:6 * BANK + T], rowsum[:, :], upto[:, :], start=True,
                      stop=True).then_inc(cum_done, 1)
            pe.wait_ge(bad_ready, 1)
            pe.matmul(acc[0:1, 6 * BANK + 64:6 * BANK + 65], bad[:, 2:3], ones_col[:, :], start=True, stop=True).then_inc(bad_done, 1)

            def clear_sums(n, bs):
                for lo, hi in bs:
                    pe.matmul(acc[0:n, lo:hi], zeros[:, 0:n], zeros[:, 0:hi - lo], start=True, stop=False,
                              skip_group_check=True)

            def chunk_sums(r):
                n = DX if r == 0 else P
                clear_sums(n, banks)
                with pe.Fori(0, HALF) as i:
                    for k in range(2):
                        if r == 0:
                            pe.wait_ge(erow_in[k], i * 16 + 16)
                            pe.wait_ge(ew_ready, 2 * i + k + 1)
                            lhs = erow[:, k, :]
                        else:
                            pe.wait_ge(msg_ready, 2 * i + k + 1 + (r - 1) * C + 2)
                            lhs = msg[:, k, :]
                        pe.wait_ge(oh_ready, 2 * i + k + 1 + r * C)
                        for lo, hi in banks:
                            mm = pe.matmul(acc[0:n, lo:hi], lhs, onehot[:, k, lo:hi], start=False, stop=False,
                                           skip_group_check=True)
                        mm.then_inc(chunk_done, 1)
                if r >= 2:
                    for t in range(T):
                        mm = pe.matmul(acc[:, t * P:(t + 1) * P], z_sb[:, t, :], ident[:, :], start=False,
                                       stop=False, skip_group_check=True)
                else:
                    mm = pe.matmul(acc[0:n, NP - P:NP], zeros[:, 0:n], zeros[:, 0:P], start=False, stop=False,
                                   skip_group_check=True)
                mm.then_inc(sum_done, 1)

            fast = sorted_fits(pe)
            with pe.If(fast):
                pe.sem_inc(built, 4)
                pe.sem_inc(row_summed, 2)
                clear_sums(P, banks[:6])

                def sum_row(tt, par):
                    t = tt * 2 + par
                    pe.wait_ge(row_ready, t + 1)
                    pe.wait_ge(h_ready, t + 1)
                    for lo, hi in banks[:6]:
                        pe.matmul(acc[:, lo:hi], hslot[:, par, :], rows[:, par, 0, lo:hi], start=False, stop=False,
                                  skip_group_check=True)

                def sum_row_last(par):
                    pe.matmul(work[0][:, 3 * P:4 * P], hslot[:, par, :], rows[:, par, 0, 6 * BANK:NP],
                              start=True, stop=True, skip_group_check=True).then_inc(row_summed, 1)

                def chunk(tt, par, j):
                    u = par * TC + j
                    s, b = u % 4, work[j % 2]
                    pe.wait_ge(ohw_ready, tt * (2 * TC) + (u + 1))
                    if j >= 2:
                        pe.wait_ge(evac, tt * (2 * T) + (par * T + j - 1))
                    elif not (isinstance(tt, int) and tt == 0 and par == 0):
                        if j == 0:
                            pe.wait_ge(evac, tt * (2 * T) + par * T)
                        else:
                            pe.wait_ge(diag_taken, tt * 2 + par)
                    if j == 4 and not (isinstance(tt, int) and tt == 0 and par == 0):
                        sum_row_last(1 - par)
                    upper = [o[:, s, :].bitcast(BF16).rearrange("p (n h) -> p n h", h=2)[:, :, 1] for o in (ohd, ohs)]
                    pe.matmul(b[:, 0:P], upper[0], upper[1], start=True, stop=True, skip_group_check=True)
                    pe.matmul(b[:, P:2 * P], ohd[:, s, :], ohw[:, s, :], start=True, stop=(j < TC - 1),
                              skip_group_check=True)
                    if j == TC - 1:
                        pe.matmul(b[:, P:2 * P], identB[:, :], identB[:, :], start=False, stop=True, skip_group_check=True)
                    pe.matmul(b[:, 2 * P:2 * P + DX], ohs[:, s, :], rec[:, par, j, 0:DX], start=True, stop=True,
                              skip_group_check=True).then_inc(built, 1)

                def tile(tt, par):
                    for j in range(TC):
                        chunk(tt, par, j)
                        if j == 3 and par:
                            sum_row(tt, 0)
                        elif j == 3 and not (isinstance(tt, int) and tt == 0):
                            sum_row(tt - 1, 1)

                build_tiles(pe, tile)
                sum_row(T // 2, 0)
                pe.wait_ge(evac, T * T)
                sum_row_last(0)
                pe.wait_ge(row_summed, T + 2)
                pe.sem_inc(sum_done, 1)
                pe.wait_ge(edge_added, T + 2)
                for g in range(-(-T // 4)):
                    if g == 0:
                        pe.wait_ge(last_added, T + 1)
                    if g >= 2:
                        pe.wait_ge(sum_copied, 6 + g - 1)
                    for t in range(4 * g, min(T, 4 * g + 4)):
                        mm = pe.transpose(work[g % 2][0:DX, (t % 4) * P:(t % 4 + 1) * P], edge_acc[:, t, :], ident[:, :])
                    mm.then_inc(edge_t, 1)
                pe.wait_ge(edge_t, -(-T // 4))
                pe.sem_inc(sum_done, 1)
            with pe.Else():
                chunk_sums(0)
                pe.wait_ge(sum_copied, NB)
                chunk_sums(1)
            pe.wait_ge(sum_copied, 2 * NB)
            for t in range(T):
                mm = pe.matmul(acc[:, 7 * BANK + t:7 * BANK + t + 1], edgeT[0:DX, t * P:(t + 1) * P], sel[0:DX, :],
                               start=True, stop=True)
            mm.then_inc(deg_done, 1)
            pe.wait_ge(weights_in, 16 * 8)
            pe.wait_ge(bias_sum, 1)
            for r in range(3):
                if r:
                    pe.wait_ge(z_ready, r + 1)
                    with pe.If(fast):
                        if r == 1:
                            pe.sem_inc(w_used, 4)
                        clear_sums(P, banks)

                        def w_tile(k, w_at, h_at):
                            pe.wait_ge(w_in[k], w_at)
                            pe.wait_ge(h_ready, h_at)
                            for lo, hi in banks:
                                mm = pe.matmul(acc[:, lo:hi], hslot[:, k, :], wslot[:, k, lo:hi], start=False,
                                               stop=False, skip_group_check=True)
                            return mm

                        with pe.Fori(0, T // 4) as q:
                            for k in range(4):
                                w_tile(k, q * 16 + (16 + (r - 1) * 16 * (T // 4 + (k == 0))),
                                       q * 4 + (k + 1 + r * T)).then_inc(w_used, 1)
                        mm = w_tile(0, 16 * r * (T // 4 + 1), (r + 1) * T)
                        mm.then_inc(w_used, 1)
                        pe.wait_ge(w_used, r * T + 4)
                        pe.sem_inc(sum_done, 1)
                    with pe.Else():
                        chunk_sums(r + 1)
                    pe.wait_ge(sum_copied, (r + 2) * NB)
                w = (wl, w1, w2)[r]
                for t in range(T):
                    cols = slice(t * P, (t + 1) * P)
                    mm = pe.matmul(acc[:, cols], sumT[:, cols], w[:, :], start=True, stop=(r > 0))
                    if r == 0:
                        mm = pe.matmul(acc[:, cols], edgeT[0:DX, cols], we[0:DX, :], start=False, stop=True)
                mm.then_inc(proj_done, 1)

        @block.vector
        def _(dve):
            chain = [0]

            def link(ins):
                chain[0] += 1
                ins.then_inc(dve_chain, 1)
                dve.wait_ge(dve_chain, chain[0])

            def wide(col):
                return col.unsqueeze(2).broadcast_to([P, T, D])

            def layer_norm_relu(r):
                for t in range(T):
                    last = dve.bn_stats(stats[:, t, :], x_sb[:, t, :])
                link(last)
                for t in range(T):
                    last = dve.bn_aggr(mv[:, t, :], stats[:, t, :])
                link(last)
                dve.tensor_scalar(std[:, :], mv[:, :, 1], EPS, None, ALU.add).then_inc(ln_var, 1)
                dve.wait_ge(ln_std, r + 1)
                link(dve.reciprocal(rstd[:, :], std[:, :]))
                link(dve.tensor_tensor(z_sb[:, :, :], x_sb[:, :, :], wide(mv[:, :, 0]), ALU.subtract))
                link(dve.tensor_tensor(z_sb[:, :, :], z_sb[:, :, :], wide(rstd[:, :]), ALU.mult))

            dve.wait_ge(pool_consts, 2)
            dve.tensor_scalar(ident[:, :], iotaF[:, :], pcol[:, :], None, ALU.is_equal)
            dve.tensor_scalar(identB[:, :], iotaF[:, :], pcol[:, :], None, ALU.is_equal)
            dve.tensor_scalar(triB[:, :], iotaF[:, :], pcol[:, :], None, ALU.is_gt)
            dve.tensor_scalar(pick[:, :], iotaF[:, 0:2 * T - 1], float(T - 1), None, ALU.is_equal)
            dve.tensor_scalar(spread[:, :, :], iotaF[0:T, 0:T].unsqueeze(2).broadcast_to([T, T, P]), pcol[0:T, :], None,
                              ALU.is_equal)
            dve.tensor_scalar(upto[:, :], iotaF[0:T, 0:T], pcol[0:T, :], None, ALU.is_ge)
            dve.tensor_scalar(sel[:, :], pcol[:, :], float(DE + 1), None, ALU.is_equal)
            dve.tensor_scalar(iotaD[:, :], iotaF[:, :], 1.0, None, ALU.add).then_inc(consts, 1)

            dve.wait_ge(lists_in, 16 * 7)
            for f in range(2):
                dve.tensor_copy(listF[:, f, :], listI[:, f, 0:LROW]).then_inc(lists_f, 1)
            dve.wait_ge(lists_t, 1)
            for f in range(3):
                last = dve.tensor_copy(metaP[:, f, :].rearrange("p (l k) -> p l k", k=K),
                                       acc[:, f * BANK:f * BANK + K * PL].rearrange("p (k l) -> p l k", k=K))
            link(last)
            S_HI, D_HI, WR, POS, S_LO, D_LO = range(6)
            for f in range(2):
                last = dve.tensor_copy(ti[:, f, :], metaP[:, f, :])
            link(last)
            dve.tensor_scalar(ti[:, 2, :], ti[:, 0, :], 7, None, ALU.arith_shift_right)
            link(dve.tensor_scalar(listI[:, 0, 0:C], ti[:, 1, :], 7, None, ALU.arith_shift_right))
            dve.tensor_copy(shiB[:, :], ti[:, 2, :])
            dve.tensor_copy(dhiB[:, :], listI[:, 0, 0:C])
            dve.tensor_copy(tf[:, S_HI, :], ti[:, 2, :]).then_inc(hi_ready, 1)
            dve.tensor_copy(tf[:, D_HI, :], listI[:, 0, 0:C]).then_inc(hi_ready, 1)
            dve.wait_ge(hi_ready, 2)
            for j in range(T):
                last = dve.tensor_scalar(oh_src[:, j, :], shiB[:, :], float(j), None, ALU.is_equal)
            last.then_inc(oh_src_ready, 1)
            for t in range(T):
                last = dve.tensor_scalar(oh_dst.rearrange("p (c t) -> p c t", t=T)[:, :, t], dhiB[:, :], float(t), None, ALU.is_equal)
            last.then_inc(oh_dst_ready, 1)
            link(dve.memset(before[:, :], 0.0))
            tot = acc[0:T, 7 * BANK:7 * BANK + C]
            dve.wait_ge(tot_done, 1)
            dve.wait_ge(pool_consts, 6)
            link(dve.tensor_copy(tf[0:T, POS, :], tot))
            link(dve.tensor_tensor_scan(tf[0:T, WR, :], ones_col[0:T, :].broadcast_to([T, C]),
                                        tf[0:T, POS, :], 0.0, ALU.mult, ALU.add))
            link(dve.tensor_tensor(tf[0:T, WR, :], tf[0:T, WR, :], tf[0:T, POS, :], ALU.subtract))
            link(dve.tensor_copy(ti[0:T, 2, :], tf[0:T, WR, :]))
            link(dve.tensor_scalar(ti[0:T, 2, :], ti[0:T, 2, :], 255, None, ALU.bitwise_and))
            dve.tensor_copy(cumB[:, :], ti[0:T, 2, :]).then_inc(cum_ready, 1)
            for j in range(T):
                dve.wait_ge(rank_done, j + 1)
                if j:
                    dve.wait_ge(rank_taken, j)
                last = dve.copy_predicated(before[:, :], oh_src[:, j, :].bitcast(mybir.dt.uint16),
                                           acc[:, (j % 4) * BANK:(j % 4) * BANK + C])
                last.then_inc(rank_taken, 1)
            dve.wait_ge(rank_taken, T)
            link(dve.tensor_copy(ti[:, 2, :], before[:, :]))
            dve.tensor_scalar(listI[:, 0, 0:C], ti[:, 2, :], P - 1, None, ALU.bitwise_and)
            link(dve.tensor_scalar(listI[:, 1, 0:C], ti[:, 2, :], P, None, ALU.bitwise_and))
            dve.tensor_copy(tf[:, WR, :], listI[:, 0, 0:C])
            dve.tensor_copy(tf[:, POS, :], listI[:, 1, 0:C])
            link(dve.tensor_tensor(before[:, :], tf[:, S_HI, :], tf[:, D_HI, :], ALU.is_equal))
            link(dve.tensor_tensor(before[:, :], before[:, :], tf[:, POS, :], ALU.mult))
            link(dve.scalar_tensor_tensor(out=tf[:, POS, :], in0=tf[:, WR, :], scalar=float(TC), in1=tf[:, S_HI, :],
                                          op0=ALU.mult, op1=ALU.add))
            link(dve.scalar_tensor_tensor(out=tf[:, POS, :], in0=tf[:, D_HI, :], scalar=float(P * TC), in1=tf[:, POS, :],
                                          op0=ALU.mult, op1=ALU.add))
            link(dve.tensor_scalar(tf[:, WR, :], tf[:, S_HI, :], -1.0, float(T), ALU.mult, ALU.add))
            link(dve.scalar_tensor_tensor(out=tf[:, WR, :], in0=before[:, :], scalar=1.0 / P, in1=tf[:, WR, :],
                                          op0=ALU.mult, op1=ALU.mult))
            link(dve.tensor_tensor(tf[:, POS, :], tf[:, POS, :], tf[:, WR, :], ALU.add))
            dve.tensor_copy(metaX[:, :, 4].bitcast(I32), tf[:, POS, :])
            dve.tensor_scalar(ti[:, 0, :], ti[:, 0, :], P - 1, None, ALU.bitwise_and)
            link(dve.tensor_scalar(ti[:, 1, :], ti[:, 1, :], P - 1, None, ALU.bitwise_and))
            dve.tensor_scalar(metaX[:, :, 3], ti[:, 1, :], 1.0, None, ALU.add)
            dve.tensor_copy(metaX[:, :, 2], ti[:, 0, :])
            link(dve.tensor_copy(metaX[:, :, 1], metaP[:, 2, :]))

            G = 5
            dve.wait_ge(x_in, 32)
            layer_norm_relu(0)
            dve.tensor_scalar(z_sb[:, :, :], z_sb[:, :, :], 0.0, None, ALU.max).then_inc(z_ready, 1)
            dve.wait_ge(pairs_done, 1)
            dve.tensor_copy(cnt[0:G * T, :], acc[0:G * T, 5 * BANK:5 * BANK + G * T]).then_inc(pairs_copied, 1)
            link(dve.memset(bad[:, :], 0.0))
            link(dve.tensor_tensor(listF[0:PL, 0, 0:LROW - 1], listF[0:PL, 1, 0:LROW - 1], listF[0:PL, 1, 1:LROW], ALU.is_gt))
            link(dve.tensor_reduce(bad[0:PL, 0:1], listF[0:PL, 0, 0:LROW - 1], mybir.AxisListType.X, ALU.add))
            link(dve.tensor_tensor(bad[0:PL - 1, 3:4], listF[0:PL - 1, 1, LROW - 1:LROW], listI[0:PL - 1, 1, LROW:LROW + 1], ALU.is_gt))
            dve.wait_ge(count_done, 1)
            dve.tensor_reduce(rowsum[:, :], acc[0:T, 4 * BANK:4 * BANK + T], mybir.AxisListType.X, ALU.add).then_inc(rowsum_ready, 1)
            link(dve.scalar_tensor_tensor(out=cnt[0:T, 0:T], in0=ident[0:T, 0:T], scalar=-float(P),
                                          in1=acc[0:T, 4 * BANK:4 * BANK + T], op0=ALU.mult, op1=ALU.add))
            link(dve.tensor_reduce(bad[0:T, 1:2], cnt[0:T, 0:T], mybir.AxisListType.X, ALU.max))
            link(dve.tensor_scalar(bad[0:T, 1:2], bad[0:T, 1:2], -float(P), 0.0, ALU.add, ALU.max))
            link(dve.tensor_tensor(bad[:, 2:3], bad[:, 0:1], bad[:, 1:2], ALU.add))
            dve.wait_ge(cum_done, 1)
            link(dve.memset(unitI[:, :], 0))
            link(dve.tensor_scalar(unitF[:, :], acc[0:1, 6 * BANK:6 * BANK + T], float(UNIT * P - 1), None, ALU.add))
            link(dve.tensor_copy(unitI[:, 1:T + 1], unitF[:, :]))
            link(dve.tensor_scalar(unitI[:, 1:T + 1], unitI[:, 1:T + 1], (UNIT * P).bit_length() - 1, None,
                                   ALU.arith_shift_right))
            link(dve.tensor_scalar(unitF[:, 0:1], unitI[:, T - 2:T - 1], float(UNITS - 2), None, ALU.is_gt))
            link(dve.tensor_tensor(bad[0:1, 2:3], bad[0:1, 2:3], unitF[:, 0:1], ALU.add))
            dve.tensor_tensor(bad[:, 2:3], bad[:, 2:3], bad[:, 3:4], ALU.add).then_inc(bad_ready, 1)
            dve.wait_ge(bad_done, 1)
            dve.tensor_scalar(flagI[:, :], acc[0:1, 6 * BANK + 64:6 * BANK + 65], 0.0, None, ALU.is_equal).then_inc(flag_ready, 1)

            dve.wait_ge(weights_in, 16 * 8)
            dve.tensor_tensor(we[DE:DE + 1, :], we[DE:DE + 1, :], be[DE:DE + 1, :], ALU.add).then_inc(bias_sum, 1)

            def take_slots(n, i, k):
                dve.tensor_copy(slotF[:, k, :], metaP[:, :, bass.ds(2 * i + k, 1)].rearrange("p f a -> p (f a)")).then_inc(ew_ready, 1)

            def one_hot(k):
                dve.tensor_scalar(onehot[:, k, :], iota_n, slotF[:, k, 0:1], None, ALU.is_equal).then_inc(oh_ready, 1)

            def weigh_rows(r):
                with dve.Fori(0, HALF) as i:
                    for k in range(2):
                        n = 2 * i + k + 1
                        dve.wait_ge(chunk_done, n + (r + 1) * C)
                        take_slots(n, i, k)
                        dve.tensor_copy(slotI[:, k, :], metaP[:, 1, bass.ds(2 * i + k, 1)]).then_inc(idx_ready, 1)
                        dve.wait_ge(ew_ready, n + (r + 1) * C)
                        one_hot(k)
                        dve.wait_ge(gath_in[k], i * 16 + 16 + r * HALF * 16)
                        dve.tensor_scalar(msg[:, k, :], gath[:, k, :], ones_col[:, :] if r == 0 else slotF[:, k, 2:3],
                                          None, ALU.mult).then_inc(msg_ready, 1)

            fast = sorted_fits(dve)
            with dve.If(fast):
                dve.memset(sumT[:, 6 * BANK:NP], 0.0)
                dve.sem_inc(edge_added, 2)
                dve.sem_inc(last_added, 1)

                def one_hots(tt, u):
                    par, j, s = (u // TC) % 2, u % TC, u % 4
                    r = rec[:, par, j, :]
                    if j == 0:
                        dve.wait_ge(rec_in[par], tt * 16 + (16 + 16 * (u // (2 * TC))))
                    dve.wait_ge(built, tt * (2 * TC) + (u + 1))
                    dve.tensor_scalar(ohd[:, s, :], iotaD[:, :], r[:, DE + 3:DE + 4], None, ALU.is_equal)
                    dve.tensor_scalar(ohs[:, s, :], iotaF[:, :], r[:, DE + 2:DE + 3], None,
                                      ALU.is_equal).then_inc(ohd_ready, 1)

                AHEAD = 3

                def tile(tt, par):
                    t = tt * 2 + par
                    for j in range(TC):
                        u = par * TC + j
                        if j == 9 and not (isinstance(tt, int) and tt == 0 and par == 0):
                            add_last(t - 1)
                        if not (isinstance(tt, int) and tt == T // 2 and j + AHEAD >= TC):
                            one_hots(tt, u + AHEAD)
                    u = par * TC + TC - 1
                    b = work[(TC - 1) % 2]
                    dve.wait_ge(built, tt * (2 * TC) + (u + 5))
                    dve.wait_ge(evac, tt * (2 * T) + (par * T + T))
                    dst_ = rows[:, par, :, bass.ds(t * P, P)]
                    dve.tensor_tensor(dst_, dst_, b[:, 0:2 * P].rearrange("p (m n) -> p m n", m=2),
                                      ALU.add).then_inc(row_ready, 1)
                    at = edge_acc[:, bass.ds(t, 1), :].rearrange("p a f -> p (a f)")
                    dve.wait_ge(edge_added, t + 2)
                    dve.tensor_tensor(at, at, b[:, 2 * P:2 * P + DX], ALU.add).then_inc(diag_taken, 1)
                    dve.wait_ge(diag_taken, t + 1)
                    dve.tensor_tensor(edge_acc[:, :, :], edge_acc[:, :, :], edge_row[:, par, :, :],
                                      ALU.add).then_inc(edge_added, 1)

                def add_last(t):
                    dve.wait_ge(last_taken, t + 1)
                    dve.tensor_tensor(sumT[:, 6 * BANK:NP], sumT[:, 6 * BANK:NP], last_row[:, :],
                                      ALU.add).then_inc(last_added, 1)

                for u in range(AHEAD):
                    one_hots(0, u)
                build_tiles(dve, tile)
                add_last(T - 1)
            with dve.Else():
                dve.sem_inc(chunk_done, 2)
                dve.wait_ge(gen_consts, 2)
                with dve.Fori(0, HALF) as i:
                    for k in range(2):
                        dve.wait_ge(chunk_done, 2 * i + k + 1)
                        take_slots(0, i, k)
                        dve.tensor_copy(erow[:, k, DE + 1:DX], metaP[:, 2, bass.ds(2 * i + k, 1)])
                        dve.wait_ge(ew_ready, 2 * i + k + 1)
                        one_hot(k)
                dve.sem_inc(msg_ready, 2)
                weigh_rows(0)
            dve.wait_ge(deg_done, 1)
            link(dve.tensor_scalar(deg[:, :], acc[:, 7 * BANK:7 * BANK + T], 1.0, None, ALU.add))
            link(dve.tensor_scalar(dinv[:, :], deg[:, :], 0.0, None, ALU.is_gt))
            dve.tensor_scalar(deg[:, :], deg[:, :], 1e-30, None, ALU.max).then_inc(deg_safe, 1)
            dve.wait_ge(deg_sqrt, 1)
            link(dve.reciprocal(degpos[:, :], degpos[:, :]))
            link(dve.tensor_tensor(dinv[:, :], dinv[:, :], degpos[:, :], ALU.mult))
            for r in range(3):
                if r:
                    with dve.If(1 - fast):
                        weigh_rows(r)
                dve.wait_ge(proj_done, r + 1)
                proj = acc[:, 0:NP].rearrange("p (t f) -> p t f", f=D)
                if r == 0:
                    link(dve.scalar_tensor_tensor(out=x_sb[:, :, :], in0=proj, scalar=0.0, in1=x_sb[:, :, :],
                                                  op0=ALU.max, op1=ALU.add))
                    layer_norm_relu(1)
                    link(dve.tensor_scalar(z_sb[:, :, :], z_sb[:, :, :], 0.0, None, ALU.max))
                    dve.tensor_tensor(z_sb[:, :, :], z_sb[:, :, :], wide(dinv[:, :]), ALU.mult).then_inc(z_ready, 1)
                    continue
                bias = (b1s, b2s)[r - 1][:, :].unsqueeze(1).broadcast_to([P, T, D])
                link(dve.tensor_tensor(z_sb[:, :, :], proj, wide(dinv[:, :]), ALU.mult))
                link(dve.tensor_tensor(z_sb[:, :, :], z_sb[:, :, :], bias, ALU.add))
                if r == 1:
                    link(dve.tensor_scalar(z_sb[:, :, :], z_sb[:, :, :], 0.0, None, ALU.max))
                    dve.tensor_tensor(z_sb[:, :, :], z_sb[:, :, :], wide(dinv[:, :]), ALU.mult).then_inc(z_ready, 1)
                else:
                    dve.tensor_tensor(z_sb[:, :, :], z_sb[:, :, :], x_sb[:, :, :], ALU.add).then_inc(out_ready, 1)


_INS = ['x', 'src', 'dst', 'edge_attr_64', 'edge_weight', 'L0_gnn_W_lin', 'L0_gnn_b_lin', 'L0_gnn_W_edge',
        'L0_gnn_b_edge', 'L1_gnn_W1', 'L1_gnn_b1', 'L1_gnn_W2', 'L1_gnn_b2']


def kernel(**inputs):
    import numpy as _np
    import concourse.bacc as _bacc
    from concourse import mybir as _mybir
    from concourse.bass_utils import run_bass_kernel_spmd as _run

    nc = _bacc.Bacc("TRN2", target_bir_lowering=False, num_devices=1)
    arrays, args = {}, []
    for name in _INS:
        a = _np.ascontiguousarray(inputs[name])
        arrays[f"in_{name}_dram"] = a
        args.append(nc.dram_tensor(f"in_{name}_dram", a.shape, _mybir.dt.from_np(a.dtype), kind="ExternalInput").ap())
    out = nc.dram_tensor("out_dram", inputs["x"].shape, _mybir.dt.float32, kind="ExternalOutput").ap()
    build_graph_layers(nc, *args, out)
    r = _run(nc, [arrays], core_ids=[0])
    return r.results[0]["out_dram"]
```

```python
from contextlib import ExitStack

import concourse.bass as bass
from concourse import mybir

F32 = mybir.dt.float32
BF16 = mybir.dt.bfloat16
I32 = mybir.dt.int32
ALU = mybir.AluOpType
ACT = mybir.ActivationFunctionType

P = 128
BANK = 512


def build_graph_layers(nc, x, src, dst, edge_attr, edge_weight, W_lin, b_lin, W_edge, b_edge,
                       W1, b1, W2, b2, out):
    N, D = x.shape
    E, DE = edge_attr.shape
    T = -(-N // P)
    NP = T * P
    NR = N - (T - 1) * P
    C = -(-E // P)
    ER = E - (C - 1) * P
    K = 4
    PL = C // K
    LROW = K * P
    LR = E - (PL - 1) * LROW
    DX = DE + 2
    NB = -(-NP // BANK)
    EPS = 1e-5
    assert C % K == 0 and PL <= P and D == P and DX <= P

    TC = T + 1
    MX = 6
    REC = DE + MX
    STG = 4
    NSTG = 4
    UNIT = STG * NSTG
    UNITS = C // UNIT
    assert C % UNIT == 0 and T % 2 == 1

    table = nc.dram_tensor("node_table", [NP, D], F32, kind="Internal").ap()
    records = nc.dram_tensor("records", [T * P * TC, REC], F32, kind="Internal").ap()
    wmat = nc.dram_tensor("wmat", [NP, N], F32, kind="Internal").ap()

    with ExitStack() as ctx:
        def sb(name, shape, dt=F32):
            return ctx.enter_context(nc.sbuf_tensor(name, shape, dt))

        def sem(name):
            return ctx.enter_context(nc.semaphore(name))

        def psum(name, shape, dt=F32):
            return ctx.enter_context(nc.psum_tensor(name, shape, dt))

        x_sb = sb("x_sb", [P, T, D])
        z_sb = sb("z_sb", [P, T, D])
        sumT = sb("sumT", [P, NP])
        edge_buf = sb("edge_buf", [P, 2 * T * DX])
        edgeT = edge_buf[:, 0:NP]
        edge_row = edge_buf[:, :].rearrange("p (a t d) -> p a t d", a=2, t=T)
        arena = sb("arena", [P, 4 * NP])
        rows = arena[:, :].rearrange("p (a m n) -> p a m n", a=2, m=2)
        wslot = arena[:, :].rearrange("p (k n) -> p k n", k=4)
        iota_n = arena[:, 0:NP]
        onehot = arena[:, NP:3 * NP].rearrange("p (k n) -> p k n", k=2)
        arena_b = arena[:, :].bitcast(BF16)
        oh_src = arena_b[:, 0:T * C].rearrange("p (j c) -> p j c", j=T)
        oh_dst = arena_b[:, T * C:2 * T * C]
        rec = sb("rec", [P, 2, TC, REC])
        stage = sb("stage", [P, NSTG, STG, REC])
        metaX = sb("metaX", [P, C, MX])
        metaP = sb("metaP", [P, 3, C])
        edge_acc = sb("edge_acc", [P, T, DX])
        last_row = sb("last_row", [P, NR])
        ohd = sb("ohd", [P, 4, P])
        ohs = sb("ohs", [P, 4, P])
        ohw = sb("ohw", [P, 4, P])
        second = sb("second", [P, 2, 2 * P + DX])
        hslot = sb("hslot", [P, 4, D])
        iotaF = sb("iotaF", [P, P])
        iotaD = sb("iotaD", [P, P])
        pcol = sb("pcol", [P, 1])
        ident = sb("ident", [P, P])
        identB = sb("identB", [P, P], BF16)
        triB = sb("triB", [P, P], BF16)
        pick = sb("pick", [P, 2 * T - 1], BF16)
        spread = sb("spread", [T, T, P], BF16)
        zeros = sb("zeros", [P, BANK])
        ones_col = sb("ones_col", [P, 1])
        listI = sb("listI", [P, 2, LROW + 1], I32)
        listF = sb("listF", [P, 3, LROW])
        scratch = sb("scratch", [P, 9 * C])
        ti = scratch[:, 0:3 * C].bitcast(I32).rearrange("p (k c) -> p k c", k=3)
        tf = scratch[:, 3 * C:9 * C].rearrange("p (k c) -> p k c", k=6)
        parts = [scratch[:, q * (NP // 2):(q + 1) * (NP // 2)].bitcast(BF16) for q in range(2)]
        parts.append(sumT[:, 0:NP // 2].bitcast(BF16))
        shiB = sb("shiB", [P, C], BF16)
        dhiB = sb("dhiB", [P, C], BF16)
        cumB = sb("cumB", [T, C], BF16)
        before = sb("before", [P, C])
        bad = sb("bad", [P, 4])
        cnt = sb("cnt", [P, 5 * T])
        rowsum = sb("rowsum", [T, 1])
        upto = sb("upto", [T, T])
        wholeI = sb("wholeI", [1, 1], I32)
        heldI = sb("heldI", [1, T], I32)
        tailI = sb("tailI", [1, 2], I32)
        bufF = sb("bufF", [1, T])
        bufI = sb("bufI", [1, T], I32)
        unitF = sb("unitF", [1, T])
        unitI = sb("unitI", [1, T + 1], I32)
        flagI = sb("flagI", [1, 1], I32)
        slotF = sb("slotF", [P, 2, 3])
        slotI = sb("slotI", [P, 2, 1], I32)
        erow = sb("erow", [P, 2, DX])
        gath = sb("gath", [P, 2, D])
        msg = sb("msg", [P, 2, D])
        wl = sb("wl", [P, D])
        we = sb("we", [P, D])
        be = sb("be", [P, D])
        w1 = sb("w1", [P, D])
        w2 = sb("w2", [P, D])
        b1s = sb("b1s", [P, D])
        b2s = sb("b2s", [P, D])
        stats = sb("stats", [P, T, 6])
        mv = sb("mv", [P, T, 2])
        std = sb("std", [P, T])
        rstd = sb("rstd", [P, T])
        deg = sb("deg", [P, T])
        degpos = sb("degpos", [P, T])
        dinv = sb("dinv", [P, T])
        coef = sb("coef", [P, 2, T])
        sel = sb("sel", [P, 1])
        acc = psum("acc", [P, 8 * BANK])
        work = [acc[:, (6 + q) * BANK:(7 + q) * BANK] for q in range(2)]

        x_in = sem("x_in")
        lists_in = sem("lists_in")
        weights_in = sem("weights_in")
        pads_set = sem("pads_set")
        pool_consts = sem("pool_consts")
        consts = sem("consts")
        zeros_out = [sem(f"zeros_out{k}") for k in range(2)]
        bias_sum = sem("bias_sum")
        lists_f = sem("lists_f")
        lists_t = sem("lists_t")
        hi_ready = sem("hi_ready")
        oh_src_ready = sem("oh_src_ready")
        oh_dst_ready = sem("oh_dst_ready")
        tot_done = sem("tot_done")
        cum_ready = sem("cum_ready")
        rank_done = sem("rank_done")
        rank_taken = sem("rank_taken")
        pairs_done = sem("pairs_done")
        pairs_copied = sem("pairs_copied")
        count_done = sem("count_done")
        bad_ready = sem("bad_ready")
        rowsum_ready = sem("rowsum_ready")
        cum_done = sem("cum_done")
        bad_done = sem("bad_done")
        flag_ready = sem("flag_ready")
        ln_var = sem("ln_var")
        ln_std = sem("ln_std")
        z_ready = sem("z_ready")
        table_out = sem("table_out")
        gen_consts = sem("gen_consts")
        erow_in = [sem(f"erow_in{k}") for k in range(2)]
        ew_ready = sem("ew_ready")
        idx_ready = sem("idx_ready")
        gath_in = [sem(f"gath_in{k}") for k in range(2)]
        msg_ready = sem("msg_ready")
        oh_ready = sem("oh_ready")
        chunk_done = sem("chunk_done")
        stage_in = [sem(f"stage_in{k}") for k in range(NSTG)]
        scattered = [sem(f"scattered{k}") for k in range(NSTG)]
        rec_in = [sem(f"rec_in{k}") for k in range(2)]
        ohd_ready = sem("ohd_ready")
        ohw_ready = sem("ohw_ready")
        built = sem("built")
        evac = sem("evac")
        rec_free = sem("rec_free")
        second_added = sem("second_added")
        edge_added = sem("edge_added")
        row_ready = sem("row_ready")
        parts_ready = sem("parts_ready")
        h_ready = sem("h_ready")
        row_summed = sem("row_summed")
        last_added = sem("last_added")
        last_taken = sem("last_taken")
        w_out = [sem(f"w_out{k}") for k in range(2)]
        w_stored = sem("w_stored")
        edge_t = sem("edge_t")
        w_in = [sem(f"w_in{k}") for k in range(4)]
        w_used = sem("w_used")
        sum_done = sem("sum_done")
        sum_copied = sem("sum_copied")
        deg_done = sem("deg_done")
        proj_done = sem("proj_done")
        rows_done = sem("rows_done")
        stats_taken = sem("stats_taken")
        coef_ready = sem("coef_ready")
        deg_safe = sem("deg_safe")
        deg_sqrt = sem("deg_sqrt")
        out_done = sem("out_done")
        dve_chain = sem("dve_chain")
        fast_chain = sem("fast_chain")
        general_chain = sem("general_chain")
        pool_turn = sem("pool_turn")

        HALF = C // 2
        ZT = T // 2 + 1
        FIRST = 1
        ZL = T - 1 - FIRST * NSTG
        WEIGHED = range(2, TC, 3)
        BY_ACT = TC - len(WEIGHED)
        STORES = 4
        EDGE_ADDS = (4, 8, 12, 16, 20)
        FROM = 3
        ADD = 1
        PIECES = 6 * 2 * 3

        def pieces_at(j):
            twos = PIECES - (TC - FROM)
            first = max(0, j - FROM) + min(max(0, j - FROM), twos)
            return list(range(first, first + (1 if j - FROM >= twos else 2))) if j >= FROM else []

        def nodes_of(j):
            return NR if j == T - 1 else P

        def upper_half(ap):
            return ap.bitcast(BF16).rearrange("p (n h) -> p n h", h=2)[:, :, 1]

        banks = [(b * BANK, min(NP, (b + 1) * BANK)) for b in range(NB)]
        block = ctx.enter_context(nc.Block())

        def group(g):
            return range(4 * g, min(T, 4 * g + 4))

        def weight_tiles(eng, body):
            body(0, 0)
            with eng.Fori(0, (T - 5) // 4) as q:
                for c in range(1, 5):
                    body(q, c)
            for c in range((T - 5) // 4 * 4 + 1, T):
                body(0, c)

        def slot_of(r, c):
            return (c + r * T) % 4

        def sorted_fits(eng):
            eng.wait_ge(flag_ready, 1)
            return eng.value_load(flagI[0:1, 0:1], min_val=0, max_val=1)

        def build_tiles(eng, body):
            for par in range(2):
                body(0, par)
            with eng.Fori(1, T // 2) as tt:
                for par in range(2):
                    body(tt, par)
            body(T // 2, 0)

        @block.sync
        def _(sp):
            full = (PL - 1) * LROW
            sp.wait_ge(pads_set, 3)
            for f, a in ((1, dst), (0, src)):
                sp.dma_start(listI[0:PL - 1, f, 0:LROW], a[0:full].rearrange("(p n) -> p n", n=LROW)).then_inc(lists_in, 16)
                sp.dma_start(listI[PL - 1:PL, f, 0:LR], a[full:E].rearrange("(p n) -> p n", p=1)).then_inc(lists_in, 16)
            sp.dma_start(listI[0:PL - 1, 1, LROW:LROW + 1],
                         dst[LROW:full + 1:LROW].rearrange("(p n) -> p n", n=1),
                         allow_slow_non_contiguous=True).then_inc(lists_in, 16)
            sp.dma_start(listF[0:PL - 1, 2, :], edge_weight[0:full].rearrange("(p n) -> p n", n=LROW)).then_inc(lists_in, 16)
            sp.dma_start(listF[PL - 1:PL, 2, 0:LR], edge_weight[full:E].rearrange("(p n) -> p n", p=1)).then_inc(lists_in, 16)
            sp.dma_start(x_sb[:, 0:T - 1, :], x[0:(T - 1) * P, :].rearrange("(t p) f -> p t f", p=P)).then_inc(x_in, 16)
            sp.wait_ge(pads_set, 6)
            sp.dma_start(x_sb[0:NR, T - 1, :], x[(T - 1) * P:N, :]).then_inc(x_in, 16)
            def zero_records(first, end):
                for t in range(first, end):
                    sp.dma_start(records[t * P * TC:(t + 1) * P * TC, :].rearrange("(p j) r -> p j r", p=P),
                                 rec[:, 1, :, :]).then_inc(zeros_out[t >= ZT], 16)

            zero_records(0, ZL)
            sp.dma_start(wl[:, :], W_lin).then_inc(weights_in, 16)
            sp.dma_start(w1[:, :], W1).then_inc(weights_in, 16)
            sp.dma_start(w2[:, :], W2).then_inc(weights_in, 16)
            sp.dma_start(we[0:DE, :], W_edge).then_inc(weights_in, 16)
            sp.dma_start(we[DE:DE + 1, :], b_lin.rearrange("(a d) -> a d", a=1)).then_inc(weights_in, 16)
            sp.dma_start(be[DE:DE + 1, :], b_edge.rearrange("(a d) -> a d", a=1)).then_inc(weights_in, 16)
            sp.dma_start(b1s[:, :], b1.rearrange("(a d) -> a d", a=1).broadcast_to([P, D])).then_inc(weights_in, 16)
            sp.dma_start(b2s[:, :], b2.rearrange("(a d) -> a d", a=1).broadcast_to([P, D])).then_inc(weights_in, 16)

            fast = sorted_fits(sp)
            with sp.If(fast):
                def stage_load(unit, k, last=False):
                    row = unit * (UNIT * P) + k * (STG * P)
                    if last:
                        at = (C - STG) * P
                        sp.dma_start(stage[:, k, 0:STG - 1, 0:DE],
                                     edge_attr[at:(C - 1) * P, :].rearrange("(c p) f -> p c f", p=P)).then_inc(stage_in[k], 16)
                        sp.dma_start(stage[0:ER, k, STG - 1, 0:DE], edge_attr[(C - 1) * P:E, :]).then_inc(stage_in[k], 16)
                    else:
                        sp.dma_start(stage[:, k, :, 0:DE],
                                     edge_attr[bass.ds(row, STG * P), :].rearrange("(c p) f -> p c f", p=P)).then_inc(stage_in[k], 16)
                    sp.dma_start(stage[:, k, :, DE:REC],
                                 metaX[:, bass.ds(unit * UNIT + k * STG, STG), :]).then_inc(stage_in[k], 16)

                for k in range(NSTG):
                    stage_load(0, k)
                zero_records(ZL, ZL + 1)
                for n in range(FIRST):
                    for k in range(NSTG):
                        sp.wait_ge(scattered[k], (n + 1) * 16 * STG)
                        stage_load(n + 1, k)
                        z = ZL + 1 + n * NSTG + k
                        zero_records(z, z + 1)
                def refill(n, ks):
                    for k in ks:
                        sp.wait_ge(scattered[k], n * (16 * STG) + 16 * STG)
                        stage_load(n + 1, k)

                def next_units(first, end):
                    with sp.If(first < end):
                        with sp.Fori(first, end) as n:
                            refill(n, range(NSTG))

                def unit(t):
                    return sp.value_load(unitI[0:1, bass.ds(t, 1)], min_val=0, max_val=UNITS - 2)

                def load_records(t, par):
                    if par:
                        for z, n in zip(zeros_out, (ZT, T - ZT)):
                            sp.wait_ge(z, 16 * n)
                    sp.wait_ge(rec_free, t + 1)
                    at = records[bass.ds(t * (P * TC), P * TC), :].rearrange("(p j) r -> p j r", p=P)
                    sp.dma_start(rec[:, par, :, :], at).then_inc(rec_in[par], 16)

                def tile_records(t, par):
                    first, end = unit(t), unit(t + 1)
                    with sp.If(first < end):
                        next_units(first, end - 1)
                        held = sp.value_load(heldI[0:1, bass.ds(t, 1)], min_val=1, max_val=NSTG)
                        for k in range(NSTG):
                            refill(end - 1, [k])
                            with sp.If(held == k + 1):
                                load_records(t, par)
                    with sp.Else():
                        load_records(t, par)

                with sp.Fori(0, (T - 3) // 2) as tt:
                    for par in range(2):
                        tile_records(tt * 2 + par, par)
                next_units(unit(T - 3), UNITS - 2)
                ends = [sp.value_load(tailI[0:1, q:q + 1], min_val=1, max_val=2 * NSTG) for q in range(2)]
                for n in range(2 * NSTG):
                    k = n % NSTG
                    sp.wait_ge(scattered[k], (UNITS - 1 + n // NSTG) * 16 * STG)
                    if n < NSTG:
                        stage_load(UNITS - 1, k, last=(k == NSTG - 1))
                    for q, end in enumerate(ends):
                        with sp.If(end == n + 1):
                            load_records(T - 3 + q, (T - 3 + q) % 2)
                load_records(T - 1, (T - 1) % 2)

                sp.wait_ge(w_stored, 1)
                sp.wait_ge(sum_done, 1)
                for r in range(2):
                    def load_weights(q, c):
                        k = slot_of(r, c)
                        sp.wait_ge(w_used, q * 4 + (c + 1 + r * T))
                        sp.dma_start(wslot[:, k, 0:N], wmat[bass.ds(q * (4 * P) + c * P, P), :]).then_inc(w_in[k], 16)
                    weight_tiles(sp, load_weights)
            with sp.Else():
                for z, n in zip(zeros_out, (ZT, ZL - ZT)):
                    sp.wait_ge(z, 16 * n)
                sp.wait_ge(gen_consts, 2)
                with sp.Fori(0, HALF - 1) as i:
                    for k in range(2):
                        sp.wait_ge(chunk_done, 2 * i + k + 1)
                        sp.dma_start(erow[:, k, 0:DE], edge_attr[bass.ds(i * (2 * P) + k * P, P), :]).then_inc(erow_in[k], 16)
                sp.wait_ge(chunk_done, C - 1)
                sp.dma_start(erow[:, 0, 0:DE], edge_attr[(C - 2) * P:(C - 1) * P, :]).then_inc(erow_in[0], 16)
                sp.wait_ge(chunk_done, C)
                sp.dma_start(erow[0:ER, 1, 0:DE], edge_attr[(C - 1) * P:E, :]).then_inc(erow_in[1], 16)
                for r in range(3):
                    sp.wait_ge(z_ready, r + 1)
                    if r:
                        sp.wait_ge(sum_done, (r + 1) * NB)
                    sp.dma_start(table.rearrange("(t p) f -> p t f", p=P), z_sb[:, :, :]).then_inc(table_out, 16)
                    sp.wait_ge(table_out, 16 * (r + 1))
            for g in range(NB):
                sp.wait_ge(rows_done, 2 * NB + g + 1)
                lo, hi = group(g)[0], group(g)[-1] + 1
                if hi == T:
                    sp.dma_start(out[(T - 1) * P:N, :], z_sb[0:NR, T - 1, :]).then_inc(out_done, 16)
                else:
                    sp.dma_start(out[lo * P:hi * P, :].rearrange("(t p) f -> p t f", p=P), z_sb[:, lo:hi, :]).then_inc(out_done, 16)
            sp.wait_ge(out_done, 16 * NB)

        @block.gpsimd
        def _(pool):
            pool.memset(listI[:, 0, :], -1).then_inc(pads_set, 1)
            pool.memset(listI[:, 1, :], N - 1).then_inc(pads_set, 1)
            pool.memset(listF[:, 2, :], 0.0).then_inc(pads_set, 1)
            pool.iota(iotaF[:, :], [[1, P]], base=0, channel_multiplier=0,
                      allow_small_or_imprecise_dtypes=True).then_inc(pool_consts, 1)
            pool.iota(pcol[:, :], [[0, 1]], base=0, channel_multiplier=1,
                      allow_small_or_imprecise_dtypes=True).then_inc(pool_consts, 1)
            pool.memset(rec[:, 1, :, :], 0.0).then_inc(pads_set, 1)
            pool.memset(x_sb[:, T - 1, :], 0.0).then_inc(pads_set, 1)
            pool.memset(we[:, :], 0.0).then_inc(pads_set, 1)
            pool.memset(zeros[:, :], 0.0).then_inc(pool_consts, 1)
            pool.memset(ones_col[:, :], 1.0).then_inc(pool_consts, 1)
            pool.memset(metaX[:, :, :], 1.0).then_inc(pool_consts, 1)
            pool.memset(edge_acc[:, :, :], 0.0).then_inc(pool_consts, 1)
            fast = sorted_fits(pool)
            with pool.If(fast):
                def scatter(k, c, n=P):
                    pool.indirect_dma_start(
                        out=records[:, :], out_offset=bass.IndirectOffsetOnAxis(
                            ap=stage[0:n, k, c, DE + 4:DE + 5].bitcast(I32), axis=0),
                        in_=stage[0:n, k, c, :], in_offset=None).then_inc(scattered[k], 16)

                def scatter_units(first, end):
                    with pool.Fori(first, end) as n:
                        for k in range(NSTG):
                            pool.wait_ge(stage_in[k], n * 32 + 32)
                            pool.sem_inc(pool_turn, 1)
                            for c in range(STG):
                                scatter(k, c)

                pool.wait_ge(zeros_out[0], 16 * ZT)
                early = pool.value_load(wholeI[0:1, 0:1], min_val=0, max_val=UNITS - 2)
                with pool.If(0 < early):
                    scatter_units(0, early)
                pool.wait_ge(zeros_out[1], 16 * (T - ZT))
                scatter_units(early, UNITS - 1)
                for k in range(NSTG):
                    pool.wait_ge(stage_in[k], UNITS * 32 + (16 if k == NSTG - 1 else 0))
                    for c in range(STG):
                        scatter(k, c, ER if k == NSTG - 1 and c == STG - 1 else P)
            with pool.Else():
                pool.iota(iota_n, [[1, NP]], base=0, channel_multiplier=0,
                          allow_small_or_imprecise_dtypes=True).then_inc(gen_consts, 1)
                pool.memset(erow[:, :, :], 1.0).then_inc(gen_consts, 1)
                for r in range(3):
                    pool.wait_ge(table_out, 16 * (r + 1))
                    with pool.Fori(0, HALF) as i:
                        for k in range(2):
                            pool.wait_ge(idx_ready, 2 * i + k + 1 + r * C)
                            pool.wait_ge(msg_ready, 2 * i + k + 1 + r * C)
                            pool.sem_inc(pool_turn, 1)
                            pool.indirect_dma_start(
                                out=gath[:, k, :], out_offset=None, in_=table[:, :],
                                in_offset=bass.IndirectOffsetOnAxis(ap=slotI[:, k, :], axis=0)).then_inc(gath_in[k], 16)

        @block.scalar
        def _(act):
            act.wait_ge(ln_var, 1)
            act.activation(std[:, :], std[:, :], ACT.Sqrt).then_inc(ln_std, 1)

            def copy_sums(r, dstT, n):
                for b, (lo, hi) in enumerate(banks):
                    act.wait_ge(sum_done, r * NB + b + 1)
                    act.activation(dstT[0:n, lo:hi], acc[0:n, lo:hi], ACT.Copy).then_inc(sum_copied, 1)

            fast = sorted_fits(act)
            with act.If(fast):
                def weigh(tt, u):
                    s, j = u % 4, u % TC
                    if j in WEIGHED:
                        return
                    act.wait_ge(ohd_ready, tt * (2 * TC) + u + 1)
                    act.activation(ohw[:, s, :], ohs[:, s, :], ACT.Copy,
                                   scale=rec[:, (u // TC) % 2, j, DE + 1:DE + 2]).then_inc(ohw_ready, 1)

                AHEAD = 2

                def take_last(t):
                    act.wait_ge(last_added, t)
                    act.activation(last_row[:, :], work[0][:, 3 * P:3 * P + NR], ACT.Copy).then_inc(last_taken, 1)

                def store_row(tt, par, q):
                    if q == 0:
                        act.wait_ge(row_ready, tt * 2 + (par + 1))
                    cols = slice(q * N // STORES, (q + 1) * N // STORES)
                    act.dma_start(wmat[bass.ds(tt * (2 * P) + par * P, P), cols], rows[:, par, 1, cols]).then_inc(w_out[par], 16)

                def tile(tt, par):
                    t = tt * 2 + par
                    first = isinstance(tt, int) and tt == 0 and par == 0
                    before_ = (tt, 0) if par else (tt - 1, 1)
                    for j in range(TC):
                        u = par * TC + j
                        if not (isinstance(tt, int) and tt == T // 2 and j + AHEAD >= TC):
                            weigh(tt, u + AHEAD)
                        if j == 0:
                            act.wait_ge(row_summed, t + 1)
                            act.wait_ge(edge_added, t + 1)
                        if j % 4 == 3 and j // 4 < STORES and not first:
                            store_row(*before_, j // 4)
                        if j == TC - 1:
                            if not first:
                                act.wait_ge(w_out[1 - par], before_[0] * (16 * STORES) + 16 * STORES)
                        act.wait_ge(built, tt * (2 * TC) + (u + 5))
                        if j == 4 and not first:
                            take_last(tt * 2 + par)
                        if j == TC - 1:
                            act.activation(second[:, par, 0:2 * P], work[j % 2][:, 0:2 * P], ACT.Copy).then_inc(rec_free, 1)
                            act.activation(second[:, par, 2 * P:2 * P + DX], work[j % 2][:, 2 * P:2 * P + DX],
                                           ACT.Copy).then_inc(evac, 1)
                            continue
                        n = nodes_of(j)
                        act.activation(rows[:, par, :, j * P:j * P + n],
                                       work[j % 2][:, 0:2 * P].rearrange("p (m n) -> p m n", m=2)[:, :, 0:n], ACT.Copy)
                        act.activation(edge_row[:, par, j, :], work[j % 2][:, 2 * P:2 * P + DX], ACT.Copy).then_inc(evac, 1)

                act.sem_inc(rec_free, 2)
                for u in range(AHEAD):
                    weigh(0, u)
                build_tiles(act, tile)
                for q in range(STORES):
                    store_row(T // 2, 0, q)
                act.wait_ge(row_summed, T + 2)
                take_last(T)
                act.wait_ge(sum_done, 1)
                for g, (lo, hi) in enumerate(banks):
                    if g < NB - 1:
                        act.activation(sumT[:, lo:hi], acc[:, lo:hi], ACT.Copy).then_inc(sum_copied, 1)
                    act.wait_ge(edge_t, g + 1)
                    act.activation(edgeT[0:DX, lo:hi], work[g % 2][0:DX, 0:hi - lo], ACT.Copy).then_inc(sum_copied, 1)
                    if g == 1:
                        act.wait_ge(w_out[0], 16 * STORES * (T // 2 + 1))
                        act.sem_inc(w_stored, 1)
                act.wait_ge(sum_copied, 2 * NB - 1)
                act.sem_inc(sum_copied, 1)
            with act.Else():
                copy_sums(0, edgeT, DX)
                copy_sums(1, sumT, P)
            act.wait_ge(deg_safe, 1)
            act.activation(degpos[:, :], deg[:, :], ACT.Sqrt).then_inc(deg_sqrt, 1)
            act.wait_ge(ln_var, 2)
            act.activation(std[:, :], std[:, :], ACT.Sqrt).then_inc(ln_std, 1)
            for r in range(2):
                with act.If(fast):
                    def scale_rows(q, c):
                        k, t = slot_of(r, c), q * 4 + c
                        act.wait_ge(w_used, t + (1 + r * T))
                        if r == 0:
                            act.activation(hslot[:, k, :], row_of(x_sb, t), ACT.Relu, bias=coef[:, 1, bass.ds(t, 1)],
                                           scale=coef[:, 0, bass.ds(t, 1)]).then_inc(h_ready, 1)
                        else:
                            act.wait_ge(rows_done, q + (NB + c // 4 + 1))
                            act.activation(hslot[:, k, :], row_of(z_sb, t), ACT.Relu,
                                           scale=dinv[:, bass.ds(t, 1)]).then_inc(h_ready, 1)

                    def row_of(a, t):
                        return a[:, bass.ds(t, 1), :].rearrange("p a f -> p (a f)")

                    if r == 0:
                        act.wait_ge(coef_ready, 1)
                    weight_tiles(act, scale_rows)
                copy_sums(2 + r, sumT, P)

        @block.tensor
        def _(pe):
            pe.wait_ge(consts, 1)
            pe.wait_ge(pool_consts, 6)
            pe.wait_ge(lists_f, 2)
            for f in range(3):
                for k in range(K):
                    mm = pe.transpose(acc[:, f * BANK + k * PL:f * BANK + (k + 1) * PL],
                                      listF[0:PL, f, k * P:(k + 1) * P], ident[0:PL, 0:PL])
            mm.then_inc(lists_t, 1)
            tot = acc[0:T, 7 * BANK:7 * BANK + C]
            for j in range(T):
                pe.wait_ge(oh_src_ready, j + 1)
                mm = pe.matmul(tot, pick[:, T - 1 - j:2 * T - 1 - j], oh_src[:, j, :], start=(j == 0), stop=(j == T - 1))
            mm.then_inc(tot_done, 1)
            pe.wait_ge(cum_ready, 1)
            for j in range(T):
                if j >= 4:
                    pe.wait_ge(rank_taken, j - 3)
                o = acc[:, (j % 4) * BANK:(j % 4) * BANK + C]
                pe.matmul(o, triB[:, :], oh_src[:, j, :], start=True, stop=False)
                pe.matmul(o, spread[:, j, :], cumB[:, :], start=False, stop=True).then_inc(rank_done, 1)
            G = 5
            pairs = acc[0:G * T, 5 * BANK:5 * BANK + G * T].rearrange("p (c j) -> p c j", c=G)
            src_by_chunk = oh_src.rearrange("p j c -> p c j")
            pe.wait_ge(oh_dst_ready, 1)
            for q in range(C // G):
                pe.matmul(pairs, oh_dst[:, q * (G * T):(q + 1) * (G * T)], src_by_chunk[:, q * G:(q + 1) * G, :],
                          start=(q == 0), stop=False, skip_group_check=True)
            mm = pe.matmul(pairs[0:T, 0, :], oh_dst[:, (C - 1) * T:C * T], src_by_chunk[:, C - 1, :],
                           start=False, stop=True, skip_group_check=True)
            mm.then_inc(pairs_done, 1)
            pe.wait_ge(pairs_copied, 1)
            for g in range(G):
                mm = pe.matmul(acc[0:T, 4 * BANK:4 * BANK + T], ident[0:G * T, g * T:(g + 1) * T],
                               cnt[0:G * T, g * T:(g + 1) * T], start=(g == 0), stop=(g == G - 1))
            mm.then_inc(count_done, 1)
            pe.wait_ge(rowsum_ready, 1)
            pe.matmul(acc[0:1, 6 * BANK:6 * BANK + T], rowsum[:, :], upto[:, :], start=True,
                      stop=True).then_inc(cum_done, 1)
            pe.wait_ge(bad_ready, 1)
            pe.matmul(acc[0:1, 6 * BANK + 64:6 * BANK + 65], bad[:, 2:3], ones_col[:, :], start=True, stop=True).then_inc(bad_done, 1)

            def clear_sums(n, bs):
                for lo, hi in bs:
                    pe.matmul(acc[0:n, lo:hi], zeros[:, 0:n], zeros[:, 0:hi - lo], start=True, stop=False,
                              skip_group_check=True)

            def chunk_sums(r):
                n = DX if r == 0 else P
                clear_sums(n, banks)
                with pe.Fori(0, HALF) as i:
                    for k in range(2):
                        if r == 0:
                            pe.wait_ge(erow_in[k], i * 16 + 16)
                            pe.wait_ge(ew_ready, 2 * i + k + 1)
                            lhs = erow[:, k, :]
                        else:
                            pe.wait_ge(msg_ready, 2 * i + k + 1 + (r - 1) * C + 2)
                            lhs = msg[:, k, :]
                        pe.wait_ge(oh_ready, 2 * i + k + 1 + r * C)
                        for lo, hi in banks:
                            mm = pe.matmul(acc[0:n, lo:hi], lhs, onehot[:, k, lo:hi], start=False, stop=False,
                                           skip_group_check=True)
                        mm.then_inc(chunk_done, 1)
                if r >= 2:
                    for t in range(T):
                        mm = pe.matmul(acc[:, t * P:(t + 1) * P], z_sb[:, t, :], ident[:, :], start=False,
                                       stop=False, skip_group_check=True)
                else:
                    mm = pe.matmul(acc[0:n, NP - P:NP], zeros[:, 0:n], zeros[:, 0:P], start=False, stop=False,
                                   skip_group_check=True)
                mm.then_inc(sum_done, 1)
                pe.wait_ge(sum_done, r * NB + 1)
                pe.sem_inc(sum_done, NB - 1)

            def project(r, g):
                for t in group(g):
                    cols = slice(t * P, (t + 1) * P)
                    mm = pe.matmul(acc[:, cols], sumT[:, cols], (wl, w1, w2)[r][:, :], start=True, stop=(r > 0))
                    if r == 0:
                        mm = pe.matmul(acc[:, cols], edgeT[0:DX, cols], we[0:DX, :], start=False, stop=True)
                mm.then_inc(proj_done, 1)

            fast = sorted_fits(pe)
            with pe.If(fast):
                pe.sem_inc(built, 4)
                pe.sem_inc(row_summed, 2)
                clear_sums(P, banks[:6])
                pe.wait_ge(parts_ready, 1)

                def sum_row(t, par, n):
                    if n == 0:
                        pe.wait_ge(row_ready, t + 1)
                    lo = n // 3 * (BANK // 2)
                    hi = lo + BANK // 2
                    return pe.matmul(acc[:, lo:hi], parts[n % 3][:, bass.ds(t * P, P)], upper_half(rows[:, par, 0, lo:hi]),
                                     start=False, stop=False, skip_group_check=True)

                def sum_row_last(t, par):
                    for q in range(3):
                        mm = pe.matmul(work[0][:, 3 * P:3 * P + NR], parts[q][:, bass.ds(t * P, P)],
                                       upper_half(rows[:, par, 0, 6 * BANK:N]), start=(q == 0), stop=(q == 2),
                                       skip_group_check=True)
                    return mm

                def chunk(tt, par, j):
                    u = par * TC + j
                    s, b = u % 4, work[j % 2]
                    if j in WEIGHED:
                        pe.wait_ge(ohd_ready, tt * (2 * TC) + (u + 1))
                    else:
                        pe.wait_ge(ohw_ready, tt * (2 * BY_ACT) + (par * BY_ACT + j + 1 - sum(w < j for w in WEIGHED)))
                    pieces = []
                    if not (isinstance(tt, int) and tt == 0 and par == 0):
                        pieces = pieces_at(j)
                    for n in pieces[:1]:
                        mm = sum_row(tt * 2 + (par - 1), 1 - par, n)
                        if n == PIECES - 1:
                            mm.then_inc(row_summed, 1)
                    if not isinstance(tt, int) or tt * 2 * TC + u >= 2:
                        pe.wait_ge(evac, tt * (2 * TC) + (u - 1))
                    if j == 4 and not (isinstance(tt, int) and tt == 0 and par == 0):
                        sum_row_last(tt * 2 + (par - 1), 1 - par)
                    n = nodes_of(j)
                    pe.matmul(b[:, 0:n], upper_half(ohd[:, s, :]), upper_half(ohs[:, s, 0:n]), start=True, stop=True,
                              skip_group_check=True)
                    for piece in pieces[1:]:
                        sum_row(tt * 2 + (par - 1), 1 - par, piece)
                    pe.matmul(b[:, P:P + n], ohd[:, s, :], ohw[:, s, 0:n], start=True, stop=(j < TC - 1),
                              skip_group_check=True)
                    if j == TC - 1:
                        pe.matmul(b[:, P:2 * P], identB[:, :], identB[:, :], start=False, stop=True, skip_group_check=True)
                    pe.matmul(b[:, 2 * P:2 * P + DX], ohs[:, s, :], rec[:, par, j, 0:DX], start=True, stop=True,
                              skip_group_check=True).then_inc(built, 1)

                def tile(tt, par):
                    for j in range(TC):
                        chunk(tt, par, j)

                build_tiles(pe, tile)
                for n in range(PIECES):
                    sum_row(T - 1, 0, n)
                pe.wait_ge(evac, T * TC)
                sum_row_last(T - 1, 0).then_inc(row_summed, 1)
                pe.wait_ge(row_summed, T + 2)
                pe.sem_inc(sum_done, 2 * NB)
                pe.sem_inc(w_used, 4)
                pe.wait_ge(weights_in, 16 * 8)
                pe.wait_ge(bias_sum, 1)

                def turn_edges(g):
                    if g >= 2:
                        pe.wait_ge(sum_copied, 2 * g - 2)
                    for t in group(g):
                        mm = pe.transpose(work[g % 2][0:DX, (t % 4) * P:(t % 4 + 1) * P], edge_acc[:, t, :], ident[:, :])
                    mm.then_inc(edge_t, 1)

                pe.wait_ge(edge_added, T + 2)
                pe.wait_ge(last_added, T + 1)
                turn_edges(0)
                for g in range(NB):
                    if g + 1 < NB:
                        turn_edges(g + 1)
                    pe.wait_ge(sum_copied, min(2 * g + 2, 2 * NB - 1))
                    project(0, g)
            with pe.Else():
                chunk_sums(0)
                pe.wait_ge(sum_copied, NB)
                chunk_sums(1)
                pe.wait_ge(sum_copied, 2 * NB)
                for t in range(T):
                    mm = pe.matmul(acc[:, 7 * BANK + t:7 * BANK + t + 1], edgeT[0:DX, t * P:(t + 1) * P], sel[0:DX, :],
                                   start=True, stop=True)
                mm.then_inc(deg_done, 1)
                pe.wait_ge(weights_in, 16 * 8)
                pe.wait_ge(bias_sum, 1)
                for g in range(NB):
                    project(0, g)
            for r in range(1, 3):
                with pe.If(fast):
                    def weigh_tile(q, c):
                        k, t = slot_of(r - 1, c), q * 4 + c
                        before_ = (r - 1) * len(range(k, T, 4))
                        pe.wait_ge(w_in[k], q * 16 + 16 * (c // 4 + 1 + before_))
                        pe.wait_ge(h_ready, t + (1 + (r - 1) * T))
                        for b, (lo, hi) in enumerate(banks):
                            hi = min(hi, N)
                            first = isinstance(q, int) and t == 0
                            if first:
                                pe.wait_ge(rows_done, (r - 1) * NB + b + 1)
                            mm = pe.matmul(acc[:, lo:hi], hslot[:, k, :], wslot[:, k, lo:hi], start=first,
                                           stop=False, skip_group_check=True)
                            if isinstance(q, int) and t == T - 1:
                                mm.then_inc(sum_done, 1)
                        if not (isinstance(q, int) and t == T - 1):
                            mm.then_inc(w_used, 1)
                        else:
                            pe.wait_ge(sum_done, (r + 2) * NB)
                            pe.sem_inc(w_used, 1)

                    weight_tiles(pe, weigh_tile)
                with pe.Else():
                    pe.wait_ge(rows_done, r * NB)
                    pe.wait_ge(z_ready, r + 1)
                    chunk_sums(r + 1)
                for g in range(NB):
                    pe.wait_ge(sum_copied, (r + 1) * NB + g + 1)
                    project(r, g)

        @block.vector
        def _(dve):
            def chained(done):
                count = [0]

                def link(ins):
                    count[0] += 1
                    ins.then_inc(done, 1)
                    dve.wait_ge(done, count[0])
                return link

            link, link_fast, link_general = chained(dve_chain), chained(fast_chain), chained(general_chain)

            def wide(col):
                return col.unsqueeze(2).broadcast_to([P, T, D])

            def variances():
                dve.tensor_scalar(std[:, :], mv[:, :, 1], EPS, None, ALU.add).then_inc(ln_var, 1)

            dve.wait_ge(pool_consts, 2)
            dve.tensor_scalar(ident[:, :], iotaF[:, :], pcol[:, :], None, ALU.is_equal)
            dve.tensor_scalar(identB[:, :], iotaF[:, :], pcol[:, :], None, ALU.is_equal)
            dve.tensor_scalar(triB[:, :], iotaF[:, :], pcol[:, :], None, ALU.is_gt)
            dve.tensor_scalar(pick[:, :], iotaF[:, 0:2 * T - 1], float(T - 1), None, ALU.is_equal)
            dve.tensor_scalar(spread[:, :, :], iotaF[0:T, 0:T].unsqueeze(2).broadcast_to([T, T, P]), pcol[0:T, :], None,
                              ALU.is_equal)
            dve.tensor_scalar(upto[:, :], iotaF[0:T, 0:T], pcol[0:T, :], None, ALU.is_ge)
            dve.tensor_scalar(sel[:, :], pcol[:, :], float(DE + 1), None, ALU.is_equal)
            dve.tensor_scalar(iotaD[:, :], iotaF[:, :], 1.0, None, ALU.add).then_inc(consts, 1)

            dve.wait_ge(lists_in, 16 * 7)
            for f in range(2):
                dve.tensor_copy(listF[:, f, :], listI[:, f, 0:LROW]).then_inc(lists_f, 1)
            dve.wait_ge(lists_t, 1)
            for f in range(3):
                last = dve.tensor_copy(metaP[:, f, :].rearrange("p (l k) -> p l k", k=K),
                                       acc[:, f * BANK:f * BANK + K * PL].rearrange("p (k l) -> p l k", k=K))
            link(last)
            S_HI, D_HI, WR, POS, S_LO, D_LO = range(6)
            for f in range(2):
                last = dve.tensor_copy(ti[:, f, :], metaP[:, f, :])
            link(last)
            dve.tensor_scalar(ti[:, 2, :], ti[:, 0, :], 7, None, ALU.arith_shift_right)
            link(dve.tensor_scalar(listI[:, 0, 0:C], ti[:, 1, :], 7, None, ALU.arith_shift_right))
            dve.tensor_copy(shiB[:, :], ti[:, 2, :])
            dve.tensor_copy(dhiB[:, :], listI[:, 0, 0:C])
            dve.tensor_copy(tf[:, S_HI, :], ti[:, 2, :]).then_inc(hi_ready, 1)
            dve.tensor_copy(tf[:, D_HI, :], listI[:, 0, 0:C]).then_inc(hi_ready, 1)
            dve.wait_ge(hi_ready, 2)
            for j in range(T):
                dve.tensor_scalar(oh_src[:, j, :], shiB[:, :], float(j), None, ALU.is_equal).then_inc(oh_src_ready, 1)
            dve.wait_ge(pool_consts, 6)
            dve.tensor_scalar(ti[:, 0, :], ti[:, 0, :], P - 1, None, ALU.bitwise_and)
            dve.tensor_scalar(ti[:, 1, :], ti[:, 1, :], P - 1, None, ALU.bitwise_and)
            dve.tensor_tensor(tf[:, D_LO, :], tf[:, S_HI, :], tf[:, D_HI, :], ALU.is_equal)
            dve.tensor_scalar(tf[:, WR, :], tf[:, S_HI, :], -1.0 / P, T / P, ALU.mult, ALU.add)
            link(dve.scalar_tensor_tensor(out=tf[:, S_HI, :], in0=tf[:, D_HI, :], scalar=float(P * TC), in1=tf[:, S_HI, :],
                                          op0=ALU.mult, op1=ALU.add))
            dve.tensor_tensor(tf[:, D_LO, :], tf[:, D_LO, :], tf[:, WR, :], ALU.mult)
            dve.tensor_scalar(metaX[:, :, 3], ti[:, 1, :], 1.0, None, ALU.add)
            dve.tensor_copy(metaX[:, :, 2], ti[:, 0, :])
            link(dve.tensor_copy(metaX[:, :, 1], metaP[:, 2, :]))
            earlier = [before[:, :], tf[:, S_LO, :]]
            for e in earlier:
                last = dve.memset(e, 0.0)
            link(last)
            tot = acc[0:T, 7 * BANK:7 * BANK + C]
            dve.wait_ge(tot_done, 1)
            link(dve.tensor_copy(tf[0:T, POS, :], tot))
            link(dve.tensor_tensor_scan(tf[0:T, WR, :], ones_col[0:T, :].broadcast_to([T, C]),
                                        tf[0:T, POS, :], 0.0, ALU.mult, ALU.add))
            link(dve.tensor_tensor(tf[0:T, WR, :], tf[0:T, WR, :], tf[0:T, POS, :], ALU.subtract))
            link(dve.tensor_copy(ti[0:T, 2, :], tf[0:T, WR, :]))
            link(dve.tensor_scalar(ti[0:T, 2, :], ti[0:T, 2, :], 255, None, ALU.bitwise_and))
            dve.tensor_copy(cumB[:, :], ti[0:T, 2, :]).then_inc(cum_ready, 1)
            for j in range(T):
                dve.wait_ge(rank_done, j + 1)
                if j >= 2:
                    dve.wait_ge(rank_taken, j - 1)
                last = dve.copy_predicated(earlier[j % 2], oh_src[:, j, :].bitcast(mybir.dt.uint16),
                                           acc[:, (j % 4) * BANK:(j % 4) * BANK + C])
                last.then_inc(rank_taken, 1)
                last = dve.tensor_scalar(oh_dst.rearrange("p (c t) -> p c t", t=T)[:, :, j], dhiB[:, :], float(j), None,
                                         ALU.is_equal)
            last.then_inc(oh_dst_ready, 1)
            dve.wait_ge(rank_taken, T)
            link(dve.tensor_tensor(before[:, :], before[:, :], tf[:, S_LO, :], ALU.add))
            link(dve.tensor_copy(ti[:, 2, :], before[:, :]))
            dve.tensor_scalar(listI[:, 0, 0:C], ti[:, 2, :], P - 1, None, ALU.bitwise_and)
            link(dve.tensor_scalar(listI[:, 1, 0:C], ti[:, 2, :], P, None, ALU.bitwise_and))
            dve.tensor_copy(tf[:, WR, :], listI[:, 0, 0:C])
            link(dve.tensor_copy(tf[:, POS, :], listI[:, 1, 0:C]))
            link(dve.scalar_tensor_tensor(out=tf[:, S_HI, :], in0=tf[:, WR, :], scalar=float(TC), in1=tf[:, S_HI, :],
                                          op0=ALU.mult, op1=ALU.add))
            link(dve.tensor_tensor(tf[:, POS, :], tf[:, POS, :], tf[:, D_LO, :], ALU.mult))
            link(dve.tensor_tensor(tf[:, POS, :], tf[:, POS, :], tf[:, S_HI, :], ALU.add))
            link(dve.tensor_copy(metaX[:, :, 4].bitcast(I32), tf[:, POS, :]))

            G = 5
            link(dve.memset(bad[:, :], 0.0))
            link(dve.tensor_tensor(listF[0:PL, 0, 0:LROW - 1], listF[0:PL, 1, 0:LROW - 1], listF[0:PL, 1, 1:LROW], ALU.is_gt))
            link(dve.tensor_reduce(bad[0:PL, 0:1], listF[0:PL, 0, 0:LROW - 1], mybir.AxisListType.X, ALU.add))
            link(dve.tensor_tensor(bad[0:PL - 1, 3:4], listF[0:PL - 1, 1, LROW - 1:LROW], listI[0:PL - 1, 1, LROW:LROW + 1], ALU.is_gt))
            dve.wait_ge(pairs_done, 1)
            dve.tensor_copy(cnt[0:G * T, :], acc[0:G * T, 5 * BANK:5 * BANK + G * T]).then_inc(pairs_copied, 1)
            dve.wait_ge(count_done, 1)
            dve.tensor_reduce(rowsum[:, :], acc[0:T, 4 * BANK:4 * BANK + T], mybir.AxisListType.X, ALU.add).then_inc(rowsum_ready, 1)
            link(dve.scalar_tensor_tensor(out=cnt[0:T, 0:T], in0=ident[0:T, 0:T], scalar=-float(P),
                                          in1=acc[0:T, 4 * BANK:4 * BANK + T], op0=ALU.mult, op1=ALU.add))
            link(dve.tensor_reduce(bad[0:T, 1:2], cnt[0:T, 0:T], mybir.AxisListType.X, ALU.max))
            link(dve.tensor_scalar(bad[0:T, 1:2], bad[0:T, 1:2], -float(P), 0.0, ALU.add, ALU.max))
            link(dve.tensor_tensor(bad[:, 2:3], bad[:, 0:1], bad[:, 1:2], ALU.add))
            dve.wait_ge(cum_done, 1)
            ends = acc[0:1, 6 * BANK:6 * BANK + T]
            link(dve.memset(unitI[:, :], FIRST))
            dve.tensor_scalar(unitF[:, :], ends, float(UNIT * P - 1), float((FIRST + 2) * UNIT * P - 1), ALU.add, ALU.max)
            link(dve.tensor_scalar(bufF[:, :], ends, float(STG * P - 1), None, ALU.add))
            dve.tensor_copy(wholeI[:, :], ends[:, ZT - 1:ZT])
            dve.tensor_copy(unitI[:, 1:T + 1], unitF[:, :])
            link(dve.tensor_copy(bufI[:, :], bufF[:, :]))
            dve.tensor_scalar(unitI[:, 1:T + 1], unitI[:, 1:T + 1], (UNIT * P).bit_length() - 1, None, ALU.arith_shift_right)
            dve.tensor_scalar(wholeI[:, :], wholeI[:, :], (UNIT * P).bit_length() - 1, None, ALU.arith_shift_right)
            link(dve.tensor_scalar(bufI[:, :], bufI[:, :], (STG * P).bit_length() - 1, None, ALU.arith_shift_right))
            dve.tensor_scalar(tailI[:, :], bufI[:, T - 3:T - 1], -(UNITS - 2) * NSTG, 1, ALU.add, ALU.max)
            link(dve.scalar_tensor_tensor(out=heldI[:, :], in0=unitI[:, 1:T + 1], scalar=-float(NSTG), in1=bufI[:, :],
                                          op0=ALU.mult, op1=ALU.add))
            dve.tensor_scalar(heldI[:, :], heldI[:, :], NSTG, 1, ALU.add, ALU.max)
            link(dve.tensor_scalar(unitF[:, 0:1], unitI[:, T - 3:T - 2], float(UNITS - 2), None, ALU.is_gt))
            link(dve.tensor_tensor(bad[0:1, 2:3], bad[0:1, 2:3], unitF[:, 0:1], ALU.add))
            dve.tensor_tensor(bad[:, 2:3], bad[:, 2:3], bad[:, 3:4], ALU.add).then_inc(bad_ready, 1)
            dve.wait_ge(bad_done, 1)
            dve.tensor_scalar(flagI[:, :], acc[0:1, 6 * BANK + 64:6 * BANK + 65], 0.0, None, ALU.is_equal).then_inc(flag_ready, 1)

            dve.wait_ge(x_in, 32)
            for t in range(T):
                last = dve.bn_stats(stats[:, t, :], x_sb[:, t, :])
            link(last)
            for t in range(T):
                last = dve.bn_aggr(mv[:, t, :], stats[:, t, :])
            link(last)
            variances()
            dve.wait_ge(ln_std, 1)
            link(dve.reciprocal(rstd[:, :], std[:, :]))
            link(dve.tensor_tensor(z_sb[:, :, :], x_sb[:, :, :], wide(mv[:, :, 0]), ALU.subtract))
            link(dve.tensor_tensor(z_sb[:, :, :], z_sb[:, :, :], wide(rstd[:, :]), ALU.mult))
            dve.tensor_scalar(z_sb[:, :, :], z_sb[:, :, :], 0.0, None, ALU.max).then_inc(z_ready, 1)

            dve.wait_ge(weights_in, 16 * 8)
            dve.tensor_tensor(we[DE:DE + 1, :], we[DE:DE + 1, :], be[DE:DE + 1, :], ALU.add).then_inc(bias_sum, 1)

            def take_slots(n, i, k):
                dve.tensor_copy(slotF[:, k, :], metaP[:, :, bass.ds(2 * i + k, 1)].rearrange("p f a -> p (f a)")).then_inc(ew_ready, 1)

            def one_hot(k):
                dve.tensor_scalar(onehot[:, k, :], iota_n, slotF[:, k, 0:1], None, ALU.is_equal).then_inc(oh_ready, 1)

            def weigh_rows(r):
                with dve.Fori(0, HALF) as i:
                    for k in range(2):
                        n = 2 * i + k + 1
                        dve.wait_ge(chunk_done, n + (r + 1) * C)
                        take_slots(n, i, k)
                        dve.tensor_copy(slotI[:, k, :], metaP[:, 1, bass.ds(2 * i + k, 1)]).then_inc(idx_ready, 1)
                        dve.wait_ge(ew_ready, n + (r + 1) * C)
                        one_hot(k)
                        dve.wait_ge(gath_in[k], i * 16 + 16 + r * HALF * 16)
                        dve.tensor_scalar(msg[:, k, :], gath[:, k, :], ones_col[:, :] if r == 0 else slotF[:, k, 2:3],
                                          None, ALU.mult).then_inc(msg_ready, 1)

            fast = sorted_fits(dve)
            with dve.If(fast):
                dve.memset(sumT[:, 6 * BANK:NP], 0.0)
                dve.memset(wslot[:, :, N:NP], 0.0)
                dve.wait_ge(z_ready, 1)
                rowsF = z_sb[:, :, :].rearrange("p t f -> p (t f)")
                for q in range(2):
                    link_fast(dve.tensor_copy(parts[q], rowsF))
                    link_fast(dve.tensor_tensor(rowsF, rowsF, parts[q], ALU.subtract))
                dve.tensor_copy(parts[2], rowsF).then_inc(parts_ready, 1)
                dve.sem_inc(edge_added, 2)
                dve.sem_inc(last_added, 1)

                def one_hots(tt, u):
                    par, j, s = (u // TC) % 2, u % TC, u % 4
                    r = rec[:, par, j, :]
                    if j == 0:
                        dve.wait_ge(rec_in[par], tt * 16 + (16 + 16 * (u // (2 * TC))))
                    dve.wait_ge(built, tt * (2 * TC) + (u + 1))
                    dve.tensor_scalar(ohd[:, s, :], iotaD[:, :], r[:, DE + 3:DE + 4], None, ALU.is_equal)
                    ins = dve.tensor_scalar(ohs[:, s, :], iotaF[:, :], r[:, DE + 2:DE + 3], None, ALU.is_equal)
                    if j in WEIGHED:
                        ins = dve.tensor_scalar(ohw[:, s, :], iotaF[:, :], r[:, DE + 2:DE + 3], r[:, DE + 1:DE + 2],
                                                ALU.is_equal, ALU.mult)
                    ins.then_inc(ohd_ready, 1)

                AHEAD = 3

                def tile(tt, par):
                    t = tt * 2 + par
                    for j in range(TC):
                        u = par * TC + j
                        first = isinstance(tt, int) and tt == 0 and par == 0
                        if j == 9 and not first:
                            add_last(t - 1)
                        if j == ADD and not first:
                            add_second(t - 1, 1 - par)
                        if j in EDGE_ADDS and not first:
                            add_edges(t - 1, 1 - par, EDGE_ADDS.index(j))
                        if not (isinstance(tt, int) and tt == T // 2 and j + AHEAD >= TC):
                            one_hots(tt, u + AHEAD)
                def add_second(t, par):
                    dve.wait_ge(evac, t * TC + TC)
                    at = rows[:, par, :, bass.ds(t * P, P)]
                    dve.tensor_tensor(at, at, second[:, par, 0:2 * P].rearrange("p (m n) -> p m n", m=2),
                                      ALU.add).then_inc(row_ready, 1)
                    at = edge_acc[:, bass.ds(t, 1), :].rearrange("p a f -> p (a f)")
                    dve.wait_ge(edge_added, t + 2)
                    dve.tensor_tensor(at, at, second[:, par, 2 * P:2 * P + DX], ALU.add).then_inc(second_added, 1)

                def add_edges(t, par, q):
                    part = slice(q * T // len(EDGE_ADDS), (q + 1) * T // len(EDGE_ADDS))
                    if q == 0:
                        dve.wait_ge(second_added, t + 1)
                    ins = dve.tensor_tensor(edge_acc[:, part, :], edge_acc[:, part, :], edge_row[:, par, part, :], ALU.add)
                    if q == len(EDGE_ADDS) - 1:
                        ins.then_inc(edge_added, 1)

                def add_last(t):
                    dve.wait_ge(last_taken, t + 1)
                    dve.tensor_tensor(sumT[:, 6 * BANK:N], sumT[:, 6 * BANK:N], last_row[:, :],
                                      ALU.add).then_inc(last_added, 1)

                for u in range(AHEAD):
                    one_hots(0, u)
                build_tiles(dve, tile)
                add_second(T - 1, 0)
                for q in range(len(EDGE_ADDS)):
                    add_edges(T - 1, 0, q)
                dve.wait_ge(edge_added, T + 2)
                link_fast(dve.tensor_scalar(deg[:, :], edge_acc[:, :, DE + 1], 1.0, None, ALU.add))
                add_last(T - 1)
            with dve.Else():
                dve.sem_inc(chunk_done, 2)
                dve.wait_ge(gen_consts, 2)
                with dve.Fori(0, HALF) as i:
                    for k in range(2):
                        dve.wait_ge(chunk_done, 2 * i + k + 1)
                        take_slots(0, i, k)
                        dve.tensor_copy(erow[:, k, DE + 1:DX], metaP[:, 2, bass.ds(2 * i + k, 1)])
                        dve.wait_ge(ew_ready, 2 * i + k + 1)
                        one_hot(k)
                dve.sem_inc(msg_ready, 2)
                weigh_rows(0)
                dve.wait_ge(deg_done, 1)
                link_general(dve.tensor_scalar(deg[:, :], acc[:, 7 * BANK:7 * BANK + T], 1.0, None, ALU.add))
            link(dve.tensor_scalar(dinv[:, :], deg[:, :], 0.0, None, ALU.is_gt))
            dve.tensor_scalar(deg[:, :], deg[:, :], 1e-30, None, ALU.max).then_inc(deg_safe, 1)

            def proj(g):
                lo, hi = banks[g]
                return acc[:, lo:hi].rearrange("p (t f) -> p t f", f=D)

            def of(a, g):
                return a[:, group(g)[0]:group(g)[-1] + 1, :]

            for g in range(NB + 1):
                if g < NB:
                    dve.wait_ge(proj_done, g + 1)
                    dve.scalar_tensor_tensor(out=of(x_sb, g), in0=proj(g), scalar=0.0, in1=of(x_sb, g),
                                             op0=ALU.max, op1=ALU.add).then_inc(rows_done, 1)
                if g:
                    dve.wait_ge(rows_done, g)
                    for t in group(g - 1):
                        last = dve.bn_stats(stats[:, t, :], x_sb[:, t, :])
                    last.then_inc(stats_taken, 1)
                if g > 1:
                    dve.wait_ge(stats_taken, g - 1)
                    for t in group(g - 2):
                        dve.bn_aggr(mv[:, t, :], stats[:, t, :])
            dve.wait_ge(stats_taken, NB)
            for t in group(NB - 1):
                last = dve.bn_aggr(mv[:, t, :], stats[:, t, :])
            link(last)
            variances()
            dve.wait_ge(deg_sqrt, 1)
            link(dve.reciprocal(degpos[:, :], degpos[:, :]))
            link(dve.tensor_tensor(dinv[:, :], dinv[:, :], degpos[:, :], ALU.mult))
            dve.wait_ge(ln_std, 2)
            link(dve.reciprocal(rstd[:, :], std[:, :]))
            link(dve.tensor_tensor(coef[:, 0, :], rstd[:, :], dinv[:, :], ALU.mult))
            dve.scalar_tensor_tensor(out=coef[:, 1, :], in0=mv[:, :, 0], scalar=-1.0, in1=coef[:, 0, :],
                                     op0=ALU.mult, op1=ALU.mult).then_inc(coef_ready, 1)
            with dve.If(1 - fast):
                dve.wait_ge(coef_ready, 1)
                link_general(dve.tensor_tensor(z_sb[:, :, :], x_sb[:, :, :], wide(coef[:, 0, :]), ALU.mult))
                link_general(dve.tensor_tensor(z_sb[:, :, :], z_sb[:, :, :], wide(coef[:, 1, :]), ALU.add))
                dve.tensor_scalar(z_sb[:, :, :], z_sb[:, :, :], 0.0, None, ALU.max).then_inc(z_ready, 1)
                weigh_rows(1)

            def scale_back(r, g):
                dve.wait_ge(proj_done, r * NB + g + 1)
                for t in group(g):
                    last = dve.scalar_tensor_tensor(out=z_sb[:, t, :], in0=acc[:, t * P:(t + 1) * P], scalar=dinv[:, t:t + 1],
                                                    in1=b1s[:, :] if r == 1 else x_sb[:, t, :], op0=ALU.mult, op1=ALU.add)
                last.then_inc(rows_done, 1)

            for g in range(NB):
                scale_back(1, g)
            with dve.If(1 - fast):
                dve.wait_ge(rows_done, 2 * NB)
                link_general(dve.tensor_scalar(z_sb[:, :, :], z_sb[:, :, :], 0.0, None, ALU.max))
                dve.tensor_tensor(z_sb[:, :, :], z_sb[:, :, :], wide(dinv[:, :]), ALU.mult).then_inc(z_ready, 1)
                weigh_rows(2)
            link(dve.tensor_tensor(x_sb[:, :, :], x_sb[:, :, :], b2s[:, :].unsqueeze(1).broadcast_to([P, T, D]), ALU.add))
            for g in range(NB):
                scale_back(2, g)


_INS = ['x', 'src', 'dst', 'edge_attr_64', 'edge_weight', 'L0_gnn_W_lin', 'L0_gnn_b_lin', 'L0_gnn_W_edge',
        'L0_gnn_b_edge', 'L1_gnn_W1', 'L1_gnn_b1', 'L1_gnn_W2', 'L1_gnn_b2']


def kernel(**inputs):
    import numpy as _np
    import concourse.bacc as _bacc
    from concourse import mybir as _mybir
    from concourse.bass_utils import run_bass_kernel_spmd as _run

    nc = _bacc.Bacc("TRN2", target_bir_lowering=False, num_devices=1)
    arrays, args = {}, []
    for name in _INS:
        a = _np.ascontiguousarray(inputs[name])
        arrays[f"in_{name}_dram"] = a
        args.append(nc.dram_tensor(f"in_{name}_dram", a.shape, _mybir.dt.from_np(a.dtype), kind="ExternalInput").ap())
    out = nc.dram_tensor("out_dram", inputs["x"].shape, _mybir.dt.float32, kind="ExternalOutput").ap()
    build_graph_layers(nc, *args, out)
    r = _run(nc, [arrays], core_ids=[0])
    return r.results[0]["out_dram"]
```
